# Optimizing a Trainium2 kernel written in Bass

```python
import numpy as np
import jax
import jax.numpy as jnp

def _softmax(x, axis=-1):
    return jax.nn.softmax(x, axis=axis)

def _gelu(x):
    return jax.nn.gelu(x, approximate=True)

def _silu(x):
    return jax.nn.silu(x)

def _sigmoid(x):
    return jax.nn.sigmoid(x)

def _layernorm(x, axis=-1, eps=1e-05):
    m = jnp.mean(x, axis=axis, keepdims=True)
    v = jnp.var(x, axis=axis, keepdims=True)
    return (x - m) / jnp.sqrt(v + eps)

def _scatter_add(tgt, idx, src, axis=0):
    return tgt.at[idx].add(src)

def _segment_sum(src, seg, n):
    return jax.ops.segment_sum(src, seg, n)
kernel_name = 'mk_gnn_preln_d2_gnn_r64_4d4f76'

def setup_inputs(seed: int=0):
    np.random.seed(seed)
    _w = jnp.asarray

    def _rec_inputs():
        import jax
        import jax.numpy as jnp
        _gk = jax.random.key(seed)
        x = -0.0002117 + 1 * jax.random.normal(jax.random.fold_in(_gk, 1), (100000, 256), jnp.float32)
        src = jax.random.randint(jax.random.fold_in(_gk, 2), (25000,), 0, 100000, jnp.int32)
        dst = jax.random.randint(jax.random.fold_in(_gk, 3), (25000,), 0, 100000, jnp.int32)
        _o = jnp.argsort(dst, stable=True)
        src = src[_o]
        dst = dst[_o]
        edge_weight = -0.000423496 + 0.100023 * jax.random.normal(jax.random.fold_in(_gk, 13), (25000,), jnp.float32)
        return (x, src, dst, edge_weight)
    x, src, dst, edge_weight = _rec_inputs()

    def _L0_gnn_setup():
        import jax, jax.numpy as jnp
        import numpy as np
        N_NODES = 100000
        N_EDGES = 5000
        D_IN = 256
        D_H = 256
        D_OUT = 256

        def gcn_layer(x, W, b, src, dst, num_nodes):
            ones = jnp.ones(src.shape[0], dtype=x.dtype)
            deg = jax.ops.segment_sum(ones, dst, num_segments=num_nodes)
            dinv = jnp.where(deg > 0, jax.lax.rsqrt(deg), 0.0)
            norm = dinv[src] * dinv[dst]
            h = x @ W
            msg = h[src] * norm[:, None]
            out = jax.ops.segment_sum(msg, dst, num_segments=num_nodes)
            return out + b
        key = jax.random.key(seed)
        ks = jax.random.split(key, 8)
        x = jax.random.normal(ks[0], (N_NODES, D_IN), dtype=jnp.float32)
        edge_index = jax.random.randint(ks[1], (2, N_EDGES), 0, N_NODES, dtype=jnp.int64)

        def glorot(k, fan_in, fan_out):
            s = jnp.sqrt(6.0 / (fan_in + fan_out)).astype(jnp.float32)
            return jax.random.uniform(k, (fan_in, fan_out), jnp.float32, -s, s)
        return {'x': x, 'edge_index': edge_index, 'W1': glorot(ks[2], D_IN, D_H), 'b1': jnp.zeros((D_H,), jnp.float32), 'W2': glorot(ks[3], D_H, D_H), 'b2': jnp.zeros((D_H,), jnp.float32), 'W3': glorot(ks[4], D_H, D_OUT), 'b3': jnp.zeros((D_OUT,), jnp.float32)}
    _L0_gnn_all = _L0_gnn_setup()
    _L0_gnn_in = {k: v for k, v in _L0_gnn_all.items() if k in ('W1', 'b1', 'W2', 'b2', 'W3', 'b3')}
    del _L0_gnn_all

    def _L1_gnn_setup():
        import jax, jax.numpy as jnp
        import numpy as np
        BLOCK_DIMS = [8] * 32

        def _mask_indices():
            d = sum(BLOCK_DIMS)
            mask = np.ones((d, d), dtype=np.int8)
            off = 0
            for b in BLOCK_DIMS:
                mask[off:off + b, off:off + b] = 0
                off += b
            rows, cols = np.nonzero(mask)
            return (d, rows.astype(np.int32), cols.astype(np.int32))
        key = jax.random.key(seed)
        k1, k2 = jax.random.split(key)
        d, rows, cols = _mask_indices()
        N = 500000
        X = jax.random.normal(k1, (N, d), dtype=jnp.float32)
        w_est = 0.1 * jax.random.normal(k2, (rows.shape[0],), dtype=jnp.float32)
        return {'X': X, 'w_est': w_est, 'rows': jnp.asarray(rows), 'cols': jnp.asarray(cols)}
    _L1_gnn_all = _L1_gnn_setup()
    _L1_gnn_in = {k: v for k, v in _L1_gnn_all.items() if k in ()}
    del _L1_gnn_all
    return {'x': x, 'src': src, 'dst': dst, 'edge_weight': edge_weight, 'L0_gnn_W1': _L0_gnn_in['W1'], 'L0_gnn_b1': _L0_gnn_in['b1'], 'L0_gnn_W2': _L0_gnn_in['W2'], 'L0_gnn_b2': _L0_gnn_in['b2'], 'L0_gnn_W3': _L0_gnn_in['W3'], 'L0_gnn_b3': _L0_gnn_in['b3']}

def reference(x, src, dst, edge_weight, L0_gnn_W1, L0_gnn_b1, L0_gnn_W2, L0_gnn_b2, L0_gnn_W3, L0_gnn_b3):
    import jax
    import jax.numpy as jnp

    def _L0_gnn_ref(x, edge_index, W1, b1, W2, b2, W3, b3):
        import jax, jax.numpy as jnp
        import numpy as np
        N_NODES = 100000
        N_EDGES = 5000
        D_IN = 256
        D_H = 256
        D_OUT = 256

        def gcn_layer(x, W, b, src, dst, num_nodes):
            ones = jnp.ones(src.shape[0], dtype=x.dtype)
            deg = jax.ops.segment_sum(ones, dst, num_segments=num_nodes)
            dinv = jnp.where(deg > 0, jax.lax.rsqrt(deg), 0.0)
            norm = dinv[src] * dinv[dst]
            h = x @ W
            msg = h[src] * norm[:, None]
            out = jax.ops.segment_sum(msg, dst, num_segments=num_nodes)
            return out + b
        num_nodes = x.shape[0]
        loop = jnp.arange(num_nodes, dtype=edge_index.dtype)
        src = jnp.concatenate([edge_index[0], loop])
        dst = jnp.concatenate([edge_index[1], loop])
        h = gcn_layer(x, W1, b1, src, dst, num_nodes)
        h = gcn_layer(h, W2, b2, src, dst, num_nodes)
        h = gcn_layer(h, W3, b3, src, dst, num_nodes)
        return h

    def _L1_gnn_ref(X, w_est, rows, cols):
        import jax, jax.numpy as jnp
        import numpy as np
        BLOCK_DIMS = [8] * 32

        def _mask_indices():
            d = sum(BLOCK_DIMS)
            mask = np.ones((d, d), dtype=np.int8)
            off = 0
            for b in BLOCK_DIMS:
                mask[off:off + b, off:off + b] = 0
                off += b
            rows, cols = np.nonzero(mask)
            return (d, rows.astype(np.int32), cols.astype(np.int32))
        d = X.shape[1]
        W = jnp.zeros((d, d), dtype=X.dtype).at[rows, cols].set(w_est)
        return X @ W
    edge_index = jnp.stack([src, dst])
    h = jnp.maximum(_layernorm(x, axis=-1), 0.0)
    x = x + _L0_gnn_ref(h, edge_index, L0_gnn_W1, L0_gnn_b1, L0_gnn_W2, L0_gnn_b2, L0_gnn_W3, L0_gnn_b3)
    h = jnp.maximum(_layernorm(x, axis=-1), 0.0)
    x = x + _L1_gnn_ref(h, edge_weight, src, dst)
    return x

_drawn_inputs = setup_inputs


def setup_inputs(seed=0):
    import zlib

    import numpy as np

    out = dict(_drawn_inputs(seed))
    spreads = {'L0_gnn_b1': (0.0, 0.1), 'L0_gnn_b2': (0.0, 0.1), 'L0_gnn_b3': (0.0, 0.1)}
    factors = {}
    for name, (base, spread) in spreads.items():
        noise = np.random.default_rng([zlib.crc32(name.encode()), seed]).standard_normal(out[name].shape)
        drawn = base * np.exp(spread * noise) if base else spread * noise
        out[name] = jnp.asarray(drawn.astype(out[name].dtype))
    for name, factor in factors.items():
        out[name] = (out[name] * factor).astype(out[name].dtype)
    return out
```

```python
import concourse.bass as bass
from concourse import mybir
from contextlib import ExitStack

F32 = mybir.dt.float32
F16 = mybir.dt.float16
BF16 = mybir.dt.bfloat16
I32 = mybir.dt.int32
ALU = mybir.AluOpType
ACT = mybir.ActivationFunctionType

P = 128
N = 100000
D = 256
DC = D // P
E = 25000
EPS = 1e-5
ROWS = 512
DENSE = (N + ROWS - 1) // ROWS
NP_ = DENSE * ROWS
HI = NP_ // P
HC = (HI + P - 1) // P
HALF = HI // 2
PER = P - 1
TILES = 200
STEPS = TILES // 2
HT = (E + P - 1) // P
R = D + 2
SLOTS = 4
BIG = float(1 << 20)
MAGIC = 1.5 * (1 << 23)
assert STEPS % SLOTS == 0 and TILES * PER >= E and 2 * STEPS > DENSE and DENSE % SLOTS == 0


def gnn(nc, x, idx_ends, prev_ends, col_ends, row_ends, dst_nat, src_nat, weight_nat, W1, b1, W2, b2, W3, b3, out):
    ctx = ExitStack()
    with ctx:
        def sb(name, shape, dt=F32):
            return ctx.enter_context(nc.sbuf_tensor(name, shape, dt))

        def sem(name):
            return ctx.enter_context(nc.semaphore(name))

        def sems(name, n):
            return [sem(f"{name}{i}") for i in range(n)]

        node_table = nc.dram_tensor("node_table", (NP_, 2), F32).ap()
        plain = nc.dram_tensor("plain", (TILES * P, R), F32).ap()
        own_x = nc.dram_tensor("own_x", (TILES * P, D), F32).ap()
        cells = nc.dram_tensor("cells", (D * D, 1), F32).ap()
        key_rows = nc.dram_tensor("key_rows", (HT, P), F32).ap()
        V = [None] + [nc.dram_tensor(f"v{k}", (TILES * P, R), F32).ap() for k in (1, 2)]

        ident = sb("ident", [P, P])
        scanmat = sb("scanmat", [P, 2 * P + 1])
        ones = sb("ones", [P, P])
        iota = sb("iota", [P, HI], F16)
        W = [sb(f"W{k}", [P, DC, D]) for k in (1, 2, 3)]
        WT = [sb(f"WT{k}", [P, DC, D]) for k in (1, 2)]
        W23 = sb("W23", [P, DC, D])
        W123 = sb("W123", [P, DC, D])
        bcol = sb("bcol", [P, 2, DC])
        beta = sb("beta", [1, 3, D])
        beta3 = sb("beta3", [P, D])
        bsum = sb("bsum", [1, 4, D])
        bparts = sb("bparts", [1, 3, D], BF16)
        bias_rhs = sb("bias_rhs", [P, 2 * D], BF16)
        ones_b = sb("ones_b", [P, P], BF16)
        dnat = sb("dnat", [P, HT], I32)
        hilo = sb("hilo", [P, 2, HT], I32)
        hilof = sb("hilof", [P, 2, HT])
        ohi = sb("ohi", [P, SLOTS, HI], F16)
        olo = sb("olo", [P, SLOTS, P], F16)
        hist = sb("hist", [P, HC * P])
        rowtot = sb("rowtot", [P, HC])
        base = sb("base", [P, 2, HC])
        tab = sb("tab", [P, HC, P, 2])
        lb = sb("lb", [P, HC, P])
        ta = sb("ta", [P, HC, P])
        snat = sb("snat", [P, HT], I32)
        pair = sb("pair", [P, 3, HT])
        few = sb("few", [P, 1])
        inside = sb("inside", [P, 1], I32)
        key = sb("key", [P, HT])
        key_row = sb("key_row", [P, P])
        same_key = sb("same_key", [P, P])
        later = sb("later", [P, 1])
        cell = sb("cell", [P, HT], I32)
        cell_col = sb("cell_col", [P, 1], I32)
        weights = sb("weights", [P, HT])
        weight_col = sb("weight_col", [P, 1])
        Wm = sb("Wm", [P, DC, D])
        idx_ends_sb = sb("idx_ends_sb", [P, STEPS, 4], I32)
        idx_slots = sb("idx_slots", [P, STEPS, 4], I32)
        prev_sb = sb("prev_sb", [P, STEPS, 2], I32)
        col_sb = sb("col_sb", [P, TILES], I32)
        rep = sb("rep", [P, 3, STEPS, 2])
        dinv_all = sb("dinv_all", [P, TILES])
        deg_all = sb("deg_all", [P, TILES])
        xin = sb("xin", [P, SLOTS, 4, D])
        osb = sb("osb", [P, SLOTS, 4, D])
        xn = sb("xn", [P, 2, 4, D])
        hT = sb("hT", [P, 2, 2 * DC * P])
        st = sb("st", [P, 8, 6])
        diff = sb("diff", [P, 8])
        both = sb("both", [P, 8, 2])
        square = sb("square", [P, 8])
        scaled = sb("scaled", [P, 8])
        vv = sb("vv", [P, 12])
        sq = sb("sq", [P, 2, 12])
        y = sb("y", [P, 12])
        yy = sb("yy", [P, 12])
        yyv = sb("yyv", [P, 12])
        rs = sb("rs", [P, 2, 12])
        nb = sb("nb", [P, 2, 8])
        inv = sb("inv", [P, 2, 2])
        sidx = sb("sidx", [P, SLOTS, 8], I32)
        xe = sb("xe", [P, SLOTS, 4, D])
        tg = sb("tg", [P, SLOTS, 2, 2])
        msg = sb("msg", [P, SLOTS, 2, R])
        hd = sb("hd", [P, SLOTS, 2, R])
        drow = sb("drow", [P, SLOTS, 2 * P], I32)
        S = sb("S", [P, 2, 2, P])
        own = sb("own", [P, SLOTS, 2, R])
        t1 = sb("t1", [P, 2, 2, R])
        vout = sb("vout", [P, SLOTS, 2, R])
        al = sb("al", [P, 2, 2, 4])
        tT = sb("tT", [P, 2 * DC * P])
        aT = sb("aT", [P, 2 * P])
        scat = sb("scat", [P, SLOTS, 4], I32)

        bank = [ctx.enter_context(nc.psum_tensor(f"bank{i}", [P, 512], F32)) for i in range(8)]
        tp, mm, pse = bank[0:2], bank[2:4], bank[4:8]

        s_idx = sem("s_idx")
        s_w = sem("s_w")
        s_const = sem("s_const")
        s_mem = sem("s_mem")
        sp_turn = sem("sp_turn")
        s_dnat = sem("s_dnat")
        s_rows = sem("s_rows")
        s_table = sem("s_table")
        x_ld = sems("x_ld", SLOTS)
        o_st = sems("o_st", SLOTS)
        drow_ld = sems("drow_ld", SLOTS)
        plain_ld = sems("plain_ld", SLOTS)
        own_ld = sems("own_ld", SLOTS)
        plain_st = sems("plain_st", SLOTS)
        ox_st = sems("ox_st", SLOTS)
        v_st = [None, sems("v1_st", SLOTS), sems("v2_st", SLOTS)]
        xe_ld = sems("xe_ld", SLOTS)
        tg_ld = sems("tg_ld", SLOTS)
        v_ld = sems("v_ld", SLOTS)
        xd_ld = sems("xd_ld", SLOTS)
        out_sc = sems("out_sc", SLOTS)
        s_set = sem("s_set")
        s_pre = sem("s_pre")
        oh_ready = sem("oh_ready")
        oh_used = sem("oh_used")
        s_wt = sem("s_wt")
        s_beta = sem("s_beta")
        s_hist = sem("s_hist")
        s_tot = sem("s_tot")
        s_tab = sem("s_tab")
        s_rep = sem("s_rep")
        scat_ready = sem("scat_ready")
        sidx_ready = sem("sidx_ready")
        pool_turn = sem("pool_turn")
        stats_done = sem("stats_done")
        sums_done = sem("sums_done")
        squares_done = sem("squares_done")
        var_ready = sem("var_ready")
        sqrt_ready = sem("sqrt_ready")
        recip_done = sem("recip_done")
        recip2_done = sem("recip2_done")
        recip3_done = sem("recip3_done")
        diff_done = sem("diff_done")
        scaled_done = sem("scaled_done")
        rs_ready = sem("rs_ready")
        nb_ready = sem("nb_ready")
        scale_ready = sem("scale_ready")
        norm_done = sem("norm_done")
        xn_ready = sem("xn_ready")
        tp_ready = sem("tp_ready")
        hT_ready = sem("hT_ready")
        mm_ready = sem("mm_ready")
        mm_used = sem("mm_used")
        S_ready = sem("S_ready")
        carry_ready = sem("carry_ready")
        ps_ready = sem("ps_ready")
        row_copied = sem("row_copied")
        ps_used = sem("ps_used")
        inv_ready = sem("inv_ready")
        t1_ready = sem("t1_ready")
        vout_ready = sem("vout_ready")
        al_ready = sem("al_ready")
        ttp_ready = sem("ttp_ready")
        tT_ready = sem("tT_ready")
        fin_mm = sem("fin_mm")
        fin_part = sem("fin_part")
        fin_ready = sem("fin_ready")

        s_inside = sem("s_inside")
        keys_st = sem("keys_st")
        weights_ld = sem("weights_ld")
        zero_ready = sem("zero_ready")
        zero_st = sem("zero_st")
        key_ld = sem("key_ld")
        same_ready = sem("same_ready")
        later_ready = sem("later_ready")
        cell_ready = sem("cell_ready")
        cell_copied = sem("cell_copied")
        cell_st = sem("cell_st")
        wm_ld = sem("wm_ld")
        l_x = sem("l_x")
        l_stats = sem("l_stats")
        l_sums = sem("l_sums")
        l_squares = sem("l_squares")
        l_var = sem("l_var")
        l_sqrt = sem("l_sqrt")
        l_rs = sems("l_rs", 4)
        l_nb = sem("l_nb")
        l_xn = sem("l_xn")
        l_tp = sem("l_tp")
        l_hT = sem("l_hT")
        l_mm = sem("l_mm")
        l_add = sem("l_add")
        l_st = sem("l_st")

        block = ctx.enter_context(nc.Block())

        def edge_pass(s):
            return s // STEPS + 1 if 0 <= s < 3 * STEPS else 0

        def is_dense(s):
            return 0 <= s < DENSE

        def kinds(s):
            return {"edge": [edge_pass(s - l) for l in range(5)], "dense": [is_dense(s - l) for l in range(5)],
                    "first": [edge_pass(s - l) > 0 and (s - l) % STEPS == 0 for l in range(5)],
                    "begins": s // SLOTS % GS if s // SLOTS % GS < 2 else 2}

        def walk(eng, step):
            groups, g = (3 * STEPS + SLOTS) // SLOTS, 0
            while g < groups:
                same = [kinds(SLOTS * g + p) for p in range(SLOTS)]
                e = g + 1
                while e < groups and [kinds(SLOTS * e + p) for p in range(SLOTS)] == same:
                    e += 1
                if e - g == 1:
                    for p in range(SLOTS):
                        step(SLOTS * g + p, g, p, same[p])
                else:
                    with eng.Fori(g, e) as i:
                        for p in range(SLOTS):
                            step(SLOTS * i + p, i, p, same[p])
                g = e

        def back(i, p, lag):
            return (i if p >= lag else i - 1), (p - lag) % SLOTS

        def wait_past(eng, semaphore, value):
            if not isinstance(value, int) or value > 0:
                eng.wait_ge(semaphore, value)

        GS = STEPS // SLOTS

        def in_pass(s, k):
            return s - (k - 1) * STEPS

        @block.sync
        def _(sp):
            sp.dma_start(dnat[:, :], dst_nat).then_inc(s_dnat, 16)
            for tile, dram in ((idx_ends_sb, idx_ends), (prev_sb, prev_ends)):
                sp.dma_start(tile[:, :, :], dram).then_inc(s_idx, 16)
            sp.dma_start(snat[:, :], src_nat).then_inc(s_idx, 16)
            sp.dma_start(col_sb[:, :], col_ends).then_inc(s_idx, 16)
            for tile, dram in zip(W, (W1, W2, W3)):
                sp.dma_start(tile[:, :, :], dram.rearrange("(c p) n -> p c n", p=P)).then_inc(s_w, 16)
            for k, b in enumerate((b1, b2)):
                sp.dma_start(bcol[:, k, :], b).then_inc(s_w, 16)
            sp.dma_start(beta[0:1, 2, :], b3.rearrange("(a n) -> a n", a=1)).then_inc(s_w, 16)

            sp.wait_ge(s_beta, 1)
            sp.wait_ge(s_const, 3)
            for k in range(3):
                sp.dma_start(beta3[k:k + 1, :], beta[0:1, k, :]).then_inc(s_rows, 16)
                for j in range(2):
                    sp.dma_start(bias_rhs[k:k + 1, j * D:(j + 1) * D], bparts[0:1, k, :]).then_inc(s_rows, 16)
            sp.wait_ge(s_tab, 1)
            full = HI // P
            sp.dma_start(node_table[0:full * P * P, :].rearrange("(c p l) k -> p c (l k)", p=P, l=P),
                         tab[:, 0:full, :, :].rearrange("p c l k -> p c (l k)")).then_inc(s_table, 16)
            sp.dma_start(node_table[full * P * P:NP_, :].rearrange("(p l) k -> p (l k)", l=P),
                         tab[0:HI - full * P, full, :, :].rearrange("p l k -> p (l k)")).then_inc(s_table, 16)

            def wait(semaphore, value):
                sp.wait_ge(semaphore, value)
                sp.sem_inc(sp_turn, 1)

            def load_front(s, p, kd):
                row, slot_free = ROWS * s, 2 * s + 2
                k = kd["edge"][0]
                if k:
                    s1, edge_row = s + 1, 2 * P * in_pass(s, k)
                if kd["dense"][0]:
                    wait(mm_used, slot_free)
                    sp.dma_start(xin[:, p, :, :], x[bass.ds(row, ROWS), :].rearrange("(p j) d -> p j d", j=4))\
                        .then_inc(x_ld[p], 16)
                if k:
                    wait(S_ready, s1)
                    sp.dma_start(drow[:, p, :], row_ends[:, bass.ds(edge_row, 2 * P)].broadcast_to([P, 2 * P]))\
                        .then_inc(drow_ld[p], 16)

            def load_plain(s, p, k):
                slot_free, rows = 2 * s + 2, bass.ds(2 * P * in_pass(s, k), 2 * P)
                wait(ps_ready, slot_free)
                wait(plain_st[p], 16 * GS)
                sp.dma_start(msg[:, p, :, :], plain[rows, :].rearrange("(u p) r -> p u r", p=P))\
                    .then_inc(plain_ld[p], 16)

            def load_own(s, i, p, k):
                s1, rows = s + 1, bass.ds(2 * P * in_pass(s, k), 2 * P)
                stored = 16 * (i - (k - 1) * GS + 1)
                vout_read = s - 3 if k == 2 else 2 * STEPS - 4 + p + 1
                wait(v_st[k - 1][p], stored)
                wait(t1_ready, s1)
                wait(vout_ready, vout_read)
                sp.dma_start(own[:, p, :, :], V[k - 1][rows, :].rearrange("(u p) r -> p u r", p=P))\
                    .then_inc(own_ld[p], 16)

            def load_own_x(s, p):
                free, rows = in_pass(s, 3) + 1, bass.ds(2 * P * in_pass(s, 3), 2 * P)
                wait(ox_st[p], 16 * GS)
                wait(fin_ready, free)
                sp.dma_start(xe[:, p, 2:4, :], own_x[rows, :].rearrange("(u p) r -> p u r", p=P))\
                    .then_inc(xd_ld[p], 16)

            def store(s, p, k, dense):
                row, passed = ROWS * s, 2 * s + 8 + 2
                if k in (1, 2):
                    edge_row, updated = 2 * P * in_pass(s, k), s + 1
                    rows = bass.ds(edge_row, 2 * P)
                    if k == 1:
                        wait(ps_ready, passed)
                        sp.dma_start(plain[rows, :].rearrange("(u p) r -> p u r", p=P), msg[:, p, :, :])\
                            .then_inc(plain_st[p], 16)
                    wait(vout_ready, updated)
                    sp.dma_start(V[k][rows, :].rearrange("(u p) r -> p u r", p=P), vout[:, p, :, :])\
                        .then_inc(v_st[k][p], 16)
                if dense:
                    wait(mm_used, passed)
                    sp.dma_start(out[bass.ds(row, ROWS), :].rearrange("(p j) d -> p j d", j=4), osb[:, p, :, :])\
                        .then_inc(o_st[p], 16)

            def step(s, i, p, kd):
                k, k4 = kd["edge"][0], kd["edge"][4]
                load_front(s, p, kd)
                if k > 1 and k4 > 1:
                    load_plain(s, p, k)
                store(s - 4, p, k4, kd["dense"][4])
                if k > 1 and k4 <= 1:
                    load_plain(s, p, k)
                if k > 1:
                    load_own(s, i, p, k)
                if kd["edge"][2] == 3:
                    load_own_x(s - 2, back(i, p, 2)[1])
            walk(sp, step)
            for p in range(SLOTS):
                sp.wait_ge(o_st[p], 16 * (DENSE // SLOTS))
                sp.wait_ge(out_sc[p], 32 * GS)

            sp.wait_ge(s_inside, 1)
            n_inside = sp.value_load(inside[0:1, 0:1], min_val=0, max_val=E)
            with sp.If(n_inside > 0):
                sp.dma_start(weights[:, :], weight_nat).then_inc(weights_ld, 16)
                sp.dma_start(key_rows.rearrange("t p -> p t"), key[:, :], allow_slow_non_contiguous=True)\
                    .then_inc(keys_st, 16)
                sp.wait_ge(zero_ready, 1)
                sp.dma_start(cells.rearrange("(p c) a -> p (c a)", p=P), osb[:, 0, 0:2, :].rearrange("p j d -> p (j d)"))\
                    .then_inc(zero_st, 16)
                sp.wait_ge(keys_st, 16)
                with sp.Fori(0, HT) as t:
                    seen = t + 1
                    sp.dma_start(key_row[:, :], key_rows[bass.ds(t, 1), :].broadcast_to([P, P])).then_inc(key_ld, 16)
                    wait(cell_ready, seen)
                sp.wait_ge(cell_st, 16 * HT)
                sp.dma_start(Wm[:, :, :], cells.rearrange("(c p n) a -> p c (n a)", p=P, n=D)).then_inc(wm_ld, 16)
                with sp.Fori(0, DENSE) as t:
                    row, added, stored = ROWS * t, t + 1, 16 * (t + 1)
                    rows = out[bass.ds(row, ROWS), :].rearrange("(p j) d -> p j d", j=4)
                    sp.dma_start(xin[:, 0, :, :], rows).then_inc(l_x, 16)
                    wait(l_add, added)
                    sp.dma_start(rows, osb[:, 0, :, :]).then_inc(l_st, 16)
                    wait(l_st, stored)

        @block.gpsimd
        def _(pool):
            pool.memset(ident[:, :], 0.0).then_inc(s_mem, 1)
            pool.memset(scanmat[:, 0:P], 1.0).then_inc(s_mem, 1)
            pool.memset(scanmat[:, P:2 * P], 0.0).then_inc(s_mem, 1)
            pool.memset(scanmat[:, 2 * P:2 * P + 1], 1.0).then_inc(s_mem, 1)
            pool.memset(ones[:, :], 1.0).then_inc(s_mem, 1)
            pool.memset(ones_b[:, :], 1.0).then_inc(s_mem, 1)
            pool.memset(bias_rhs[:, :], 0.0).then_inc(s_mem, 1)
            pool.memset(beta3[:, :], 0.0).then_inc(s_mem, 1)
            pool.memset(aT[:, :], 0.0).then_inc(s_mem, 1)
            pool.memset(hist[:, HI:HC * P], 0.0).then_inc(s_mem, 1)
            pool.memset(msg[:, :, :, D:R], 1.0).then_inc(s_mem, 1)
            pool.memset(hd[:, :, :, D:R], 1.0).then_inc(s_mem, 1)
            pool.memset(vout[:, :, :, D:R], 0.0).then_inc(s_mem, 1)
            pool.iota(iota[:, :], [[1, HI]], base=0, channel_multiplier=0,
                      allow_small_or_imprecise_dtypes=True).then_inc(s_mem, 1)
            pool.wait_ge(s_mem, 14)
            for m in (ident[:, :], scanmat[:, P:2 * P]):
                pool.affine_select(out=m, in_=m, compare_op=ALU.not_equal, fill=1.0, base=0,
                                   pattern=[[-1, P]], channel_multiplier=1).then_inc(s_const, 1)
            pool.affine_select(out=scanmat[:, 0:P], in_=scanmat[:, 0:P], compare_op=ALU.is_gt, fill=0.0, base=0,
                               pattern=[[1, P]], channel_multiplier=-1).then_inc(s_const, 1)
            slot_bound = pool.to_reg(TILES * P - 1)
            node_bound = pool.to_reg(NP_ - 1)
            pool.wait_ge(s_table, 32)
            pool.wait_ge(s_idx, 64)
            pool.wait_ge(s_rep, 1)

            def gather(to, table, index, ready, bound=None):
                pool.indirect_dma_start(out=to, out_offset=None, in_=table,
                                        in_offset=bass.IndirectOffsetOnAxis(ap=index, axis=0),
                                        bounds_check=bound, oob_is_err=False).then_inc(ready, 16)

            def step(s, i, p, kd):
                k = kd["edge"][0]
                if k:
                    col = pool.snap(in_pass(s, k)) if not isinstance(s, int) else in_pass(s, k)
                    if k == 1:
                        wait_past(pool, xe_ld[p], 64 * i)
                        wait_past(pool, tg_ld[p], 32 * i)
                    else:
                        pool.wait_ge(xe_ld[p], 64 * GS)
                        wait_past(pool, v_ld[p], 32 * (i - GS))
                    turn()
                    if k == 1:
                        pool.tensor_copy(sidx[:, p, 0:4], idx_ends_sb[:, bass.ds(col, 1), :]
                                         .rearrange("p a k -> p (a k)")).then_inc(sidx_ready, 1)
                    else:
                        pool.sem_inc(sidx_ready, 1)
                    if k != 1:
                        pool.tensor_copy(sidx[:, p, 4:8], idx_slots[:, bass.ds(col, 1), :]
                                         .rearrange("p a k -> p (a k)")).then_inc(sidx_ready, 1)
                    else:
                        pool.sem_inc(sidx_ready, 1)
                    pool.wait_ge(sidx_ready, 2 * s + 2)
                if k == 1:
                    pool.wait_ge(norm_done, s + 1)
                    wait_past(pool, ox_st[p], 16 * i)
                    turn()
                    for u in range(2):
                        gather(tg[:, p, u, :], node_table, sidx[:, p, u:u + 1], tg_ld[p])
                    for j in range(4):
                        gather(xe[:, p, j, :], x, sidx[:, p, j:j + 1], xe_ld[p])
                if k > 1:
                    if kd["first"][0]:
                        for q in range(SLOTS):
                            pool.wait_ge(v_st[k - 1][q], 16 * GS)
                    pool.wait_ge(plain_ld[p], 16 * (i - GS + 1))
                    turn()
                    for u in range(2):
                        gather(msg[:, p, u, :], V[k - 1], sidx[:, p, 4 + u:5 + u], v_ld[p], slot_bound)
                if kd["edge"][4] == 3:
                    t = pool.snap(s - 4 - 2 * STEPS) if not isinstance(s, int) else s - 4 - 2 * STEPS
                    if kd["first"][4]:
                        for r in range(SLOTS):
                            pool.wait_ge(o_st[r], 16 * (DENSE // SLOTS))
                    wait_past(pool, out_sc[p], 32 * (i - 1 - 2 * GS))
                    turn()
                    pool.tensor_copy(scat[:, p, :], idx_slots[:, bass.ds(t, 1), :]
                                     .rearrange("p a k -> p (a k)")).then_inc(scat_ready, 1)
                    pool.wait_ge(scat_ready, t + 1)
                    pool.wait_ge(fin_ready, t + 1 + 4)
                    turn()
                    for u in range(2):
                        pool.indirect_dma_start(out=out, out_offset=bass.IndirectOffsetOnAxis(ap=scat[:, p, 2 + u:3 + u], axis=0),
                                                in_=osb[:, p, u, :], in_offset=None, bounds_check=node_bound,
                                                oob_is_err=False).then_inc(out_sc[p], 16)

            def turn():
                pool.sem_inc(pool_turn, 1)
            walk(pool, step)
            for p in range(SLOTS):
                pool.wait_ge(out_sc[p], 32 * GS)

            pool.wait_ge(s_inside, 1)
            n_inside = pool.value_load(inside[0:1, 0:1], min_val=0, max_val=E)
            with pool.If(n_inside > 0):
                cell_bound = pool.to_reg(D * D - 1)
                pool.wait_ge(weights_ld, 16)
                pool.wait_ge(zero_st, 16)
                pool.wait_ge(cell_ready, HT)
                turn()
                with pool.Fori(0, HT) as t:
                    pool.tensor_copy(cell_col[:, :], cell[:, bass.ds(t, 1)]).then_inc(cell_copied, 1)
                    pool.tensor_copy(weight_col[:, :], weights[:, bass.ds(t, 1)]).then_inc(cell_copied, 1)
                    pool.wait_ge(cell_copied, 2 * t + 2)
                    turn()
                    pool.indirect_dma_start(out=cells, out_offset=bass.IndirectOffsetOnAxis(ap=cell_col[:, 0:1], axis=0),
                                            in_=weight_col[:, 0:1], in_offset=None, bounds_check=cell_bound,
                                            oob_is_err=False).then_inc(cell_st, 16)
                    pool.wait_ge(cell_st, 16 * t + 16)
                    turn()

        @block.vector
        def _(dve):
            v = nc.vector
            count = [0]

            def link(ins):
                count[0] += 1
                ins.then_inc(s_set, 1)
                dve.wait_ge(s_set, count[0])

            dve.sem_inc(mm_used, 8)
            dve.sem_inc(S_ready, 4)
            dve.sem_inc(t1_ready, 4)
            dve.sem_inc(fin_ready, 4)

            dve.wait_ge(s_dnat, 16)
            v.tensor_scalar(hilo[:, 0, :], dnat[:, :], 7, None, ALU.logical_shift_right)
            link(v.tensor_scalar(hilo[:, 1, :], dnat[:, :], P - 1, None, ALU.bitwise_and))
            link(v.tensor_copy(hilof[:, :, :], hilo[:, :, :]))
            dve.wait_ge(s_const, 3)

            def onehots(i, j, c):
                dve.wait_ge(oh_used, 4 * i + j + 1)
                v.tensor_scalar(ohi[:, j, :], iota[:, :], hilof[:, 0, bass.ds(c, 1)], None, ALU.is_equal)
                v.tensor_scalar(olo[:, j, :], iota[:, 0:P], hilof[:, 1, bass.ds(c, 1)], None, ALU.is_equal)\
                    .then_inc(oh_ready, 1)
            with dve.Fori(0, HT // SLOTS) as i:
                for j in range(SLOTS):
                    onehots(i, j, SLOTS * i + j)

            dve.wait_ge(s_idx, 64)
            v.tensor_scalar(pair[:, 0, :], snat[:, :], D, None, ALU.min)
            link(v.tensor_scalar(pair[:, 1, :], dnat[:, :], D, None, ALU.min))
            link(v.tensor_tensor(pair[:, 2, :], pair[:, 0, :], pair[:, 1, :], ALU.max))
            link(v.scalar_tensor_tensor(pair[:, 0, :], pair[:, 0, :], float(D), pair[:, 1, :], ALU.mult, ALU.add))
            link(v.tensor_scalar(pair[:, 1, :], pair[:, 2, :], float(D), BIG, ALU.is_ge, ALU.mult))
            link(v.tensor_tensor(key[:, :], pair[:, 0, :], pair[:, 1, :], ALU.add))
            link(v.tensor_scalar(pair[:, 1, :], pair[:, 2, :], float(D), None, ALU.is_lt))
            link(v.tensor_reduce(few[:, :], pair[:, 1, :], mybir.AxisListType.X, ALU.add))
            ends = idx_ends_sb[:, :, 2:4]
            v.tensor_tensor(rep[:, 0, :, :], ends, prev_sb[:, :, :], ALU.not_equal)
            link(v.tensor_scalar(rep[:, 1, :, :], ends, -BIG, None, ALU.add))
            link(v.tensor_tensor(rep[:, 2, :, :], rep[:, 0, :, :], rep[:, 1, :, :], ALU.mult))
            v.memset(idx_slots[:, :, 0:2], 0)
            v.tensor_scalar(idx_slots[:, :, 2:4], rep[:, 2, :, :], BIG, None, ALU.add).then_inc(s_rep, 1)

            dve.wait_ge(s_pre, 1)
            v.tensor_copy(WT[1][:, :, :].rearrange("p c n -> p (c n)"), bank[0][:, :])
            link(v.tensor_copy(WT[0][:, :, :].rearrange("p c n -> p (c n)"), bank[1][:, :]))
            dve.sem_inc(s_wt, 1)
            dve.wait_ge(s_pre, 2)
            link(v.tensor_copy(W23[:, :, :].rearrange("p c n -> p (c n)"), bank[2][:, :]))
            dve.sem_inc(s_wt, 1)
            dve.wait_ge(s_pre, 3)
            v.tensor_copy(W123[:, :, :].rearrange("p c n -> p (c n)"), bank[3][:, :])
            v.tensor_copy(beta[0:1, 0, :], bank[4][0:1, 0:D])
            link(v.tensor_copy(beta[0:1, 1, :], bank[4][0:1, D:2 * D]))
            link(v.tensor_tensor(bsum[0:1, 0, :], beta[0:1, 0, :], beta[0:1, 1, :], ALU.add))
            link(v.tensor_tensor(bsum[0:1, 1, :], bsum[0:1, 0, :], beta[0:1, 2, :], ALU.add))
            for k in range(2):
                link(v.tensor_copy(bparts[0:1, k, :], bsum[0:1, 1 + k, :]))
                link(v.tensor_tensor(bsum[0:1, 2 + k, :], bsum[0:1, 1 + k, :], bparts[0:1, k, :], ALU.subtract))
            v.tensor_copy(bparts[0:1, 2, :], bsum[0:1, 3, :]).then_inc(s_beta, 1)

            half = HI // 2
            v.tensor_copy(hist[:, 0:half], bank[5][:, 0:half])
            v.tensor_copy(hist[:, half:HI], bank[6][:, 0:half]).then_inc(s_hist, 1)
            dve.wait_ge(s_pre, 4)
            for c in range(HC):
                v.tensor_copy(rowtot[:, c:c + 1], bank[c][:, 2 * P:2 * P + 1])
            link(v.tensor_copy(lb[:, 0, :], bank[0][:, 0:P]))
            dve.sem_inc(s_tot, 1)
            for c in range(HC):
                if c:
                    v.tensor_copy(lb[:, c, :], bank[c][:, 0:P])
                ins = v.tensor_copy(tab[:, c, :, 0], bank[c][:, P:2 * P])
            link(ins)
            dve.wait_ge(s_pre, 5)
            v.tensor_copy(base[:, 0, :], bank[7][:, 0:HC])
            v.tensor_copy(inside[:, :], bank[7][:, 16:17]).then_inc(s_inside, 1)
            link(v.tensor_copy(base[:, 1, :], bank[7][:, 8:8 + HC]))
            for c in range(1, HC):
                link(v.tensor_scalar(base[:, 0, c:HC], base[:, 0, c:HC], base[:, 1, c - 1:c], None, ALU.add))
            link(v.tensor_tensor(lb[:, :, :], lb[:, :, :], 
                                 base[:, 0, :].rearrange("p (c a) -> p c a", a=1).broadcast_to([P, HC, P]), ALU.add))
            link(v.tensor_scalar(ta[:, :, :], lb[:, :, :], 1.0 / PER, 0.5 / PER - 0.5, ALU.mult, ALU.add))
            link(v.tensor_scalar(ta[:, :, :], ta[:, :, :], MAGIC, -MAGIC, ALU.add, ALU.add))
            link(v.scalar_tensor_tensor(lb[:, :, :], ta[:, :, :], -float(P + PER), lb[:, :, :], ALU.mult, ALU.add))
            v.tensor_scalar(ta[:, :, :], tab[:, :, :, 0], 1.0, None, ALU.min)
            link(v.tensor_scalar(lb[:, :, :], lb[:, :, :], float((TILES - 1) * P + 1) - BIG, None, ALU.add))
            link(v.tensor_tensor(ta[:, :, :], ta[:, :, :], lb[:, :, :], ALU.mult))
            v.tensor_scalar(tab[:, :, :, 1], ta[:, :, :], BIG, None, ALU.add).then_inc(s_tab, 1)

            def named(ins, done, s):
                ins.then_inc(done, 1)
                dve.wait_ge(done, s + 1)

            def add(s, p, k):
                dve.wait_ge(mm_ready, 2 * s + k + 1)
                v.tensor_tensor(osb[:, p, 2 * k:2 * k + 2, :], mm[k][:, :].rearrange("p (j d) -> p j d", j=2),
                                xin[:, p, 2 * k:2 * k + 2, :], ALU.add).then_inc(mm_used, 1)

            def step(s, i, p, kd):
                q = p % 2
                (i1, p1), (i2, p2), (i3, p3) = (back(i, p, lag) for lag in (1, 2, 3))
                k, k2 = kd["edge"][0], kd["edge"][2]
                dense = kd["dense"][0]
                n = 8 if k == 1 else 4 if dense else 0
                hi = 12 if k2 == 1 else 10 if k == 1 else 4 if dense else 0
                if n:
                    dve.wait_ge(x_ld[p], 16 * (i + 1))
                    for j in range(4):
                        last = v.bn_stats(st[:, j, :], xin[:, p, j, :])
                    if k == 1:
                        dve.wait_ge(xe_ld[p], 64 * (i + 1))
                        for j in range(4):
                            last = v.bn_stats(st[:, 4 + j, :], xe[:, p, j, :])
                    named(last, stats_done, s)
                    v.tensor_tensor(diff[:, 0:n], st[:, 0:n, 1], st[:, 0:n, 4], ALU.subtract).then_inc(diff_done, 1)
                    v.tensor_tensor(both[:, 0:n, :], st[:, 0:n, 1:3], st[:, 0:n, 4:6], ALU.add).then_inc(sums_done, 1)
                if k == 1:
                    dve.wait_ge(tg_ld[p], 32 * (i + 1))
                    v.tensor_scalar(vv[:, 8:10], tg[:, p, :, 0], 1.0, None, ALU.add)
                if n:
                    dve.wait_ge(diff_done, s + 1)
                    v.tensor_tensor(square[:, 0:n], diff[:, 0:n], diff[:, 0:n], ALU.mult).then_inc(squares_done, 1)
                    dve.wait_ge(sums_done, s + 1)
                    v.tensor_scalar(scaled[:, 0:n], both[:, 0:n, 1], 1.0 / D, EPS, ALU.mult, ALU.add)\
                        .then_inc(scaled_done, 1)
                if k == 1:
                    v.tensor_copy(idx_slots[:, bass.ds(in_pass(s, 1), 1), 0:2].rearrange("p a k -> p (a k)"),
                                  tg[:, p, :, 1])
                if k2 == 1:
                    dve.wait_ge(carry_ready, 2 * (s - 2) + 2)
                    v.tensor_scalar(vv[:, 10:11], pse[2 * q][:, D + 1:D + 2], 1.0, None, ALU.add)
                    dve.wait_ge(ps_ready, 2 * (s - 2) + 8 + 2)
                    ins = v.tensor_scalar(vv[:, 11:12], pse[2 * q + 1][:, D + 1:D + 2], 1.0, None, ALU.add)
                if n:
                    dve.wait_ge(squares_done, s + 1)
                    dve.wait_ge(scaled_done, s + 1)
                    ins = v.scalar_tensor_tensor(vv[:, 0:n], square[:, 0:n], 0.25, scaled[:, 0:n], ALU.mult, ALU.add)
                if hi:
                    ins.then_inc(var_ready, 1)
                if kd["dense"][2]:
                    wait_past(dve, o_st[p2], 16 * i2)
                    add(s - 2, p2, 0)
                if hi:
                    dve.wait_ge(sqrt_ready, s + 1)
                    v.reciprocal(y[:, 0:hi], sq[:, q, 0:hi]).then_inc(recip_done, 1)
                if k:
                    dve.wait_ge(drow_ld[p], 16 * (i + 1))
                    dve.wait_ge(ps_ready, 2 * s + 6)
                    v.tensor_tensor(S[:, q, :, :], drow[:, p, :].rearrange("p (u e) -> p u e", u=2),
                                    col_sb[:, bass.ds(2 * in_pass(s, k), 2)].rearrange("p (u a) -> p u a", a=1)
                                    .broadcast_to([P, 2, P]), ALU.is_equal).then_inc(S_ready, 1)
                if hi:
                    dve.wait_ge(recip_done, s + 1)
                    v.scalar_tensor_tensor(yy[:, 0:hi], y[:, 0:hi], -0.5, y[:, 0:hi], ALU.mult, ALU.mult)\
                        .then_inc(recip2_done, 1)
                if hi:
                    dve.wait_ge(recip2_done, s + 1)
                    named(v.tensor_tensor(yyv[:, 0:hi], yy[:, 0:hi], vv[:, 0:hi], ALU.mult), recip3_done, s)
                    named(v.scalar_tensor_tensor(rs[:, q, 0:hi], yyv[:, 0:hi], 1.5, y[:, 0:hi], ALU.add, ALU.mult),
                          rs_ready, s)
                if k == 1:
                    v.tensor_tensor(rs[:, q, 4:6], rs[:, q, 4:6], rs[:, q, 8:10], ALU.mult).then_inc(scale_ready, 1)
                    if k2 == 1:
                        keep(s - 2, q)
                    dve.wait_ge(scale_ready, s + 1)
                elif k2 == 1:
                    keep(s - 2, q)
                if n:
                    v.scalar_tensor_tensor(nb[:, q, 0:n], both[:, 0:n, 0], -0.5, rs[:, q, 0:n], ALU.mult, ALU.mult)\
                        .then_inc(nb_ready, 1)
                if k2:
                    update(s - 2, i2, p2, q, k2, kd)
                if kd["edge"][3] == 3:
                    dve.wait_ge(xd_ld[p3], 16 * (i3 - 2 * GS + 1))
                    wait_past(dve, out_sc[p3], 32 * (i3 - 2 * GS))
                    dve.wait_ge(o_st[p3], 16 * (DENSE // SLOTS))
                    dve.wait_ge(fin_mm, in_pass(s - 3, 3) + 1)
                    for u in range(2):
                        last = v.scalar_tensor_tensor(
                            osb[:, p3, u, :], mm[p3 % 2][:, u * D:(u + 1) * D],
                            dinv_all[:, bass.ds(2 * in_pass(s - 3, 3) + u, 1)], xe[:, p3, 2 + u, :], ALU.mult, ALU.add)
                    last.then_inc(fin_ready, 1)
                if kd["dense"][2]:
                    add(s - 2, p2, 1)

            def keep(s, q):
                cols = bass.ds(2 * s, 2)
                v.tensor_copy(dinv_all[:, cols], rs[:, q, 10:12])
                v.tensor_copy(deg_all[:, cols], vv[:, 10:12])

            def update(s, i, p, q, k, kd):
                cols = bass.ds(2 * in_pass(s, k), 2)
                if k < 3:
                    wait_past(dve, vout_ready, s - 1)
                else:
                    dve.wait_ge(vout_ready, 2 * STEPS)
                    wait_past(dve, ttp_ready, in_pass(s, 3) - 1)
                if k == 1:
                    v.tensor_tensor(inv[:, q, :], rs[:, q, 10:12], rs[:, q, 10:12], ALU.mult)
                else:
                    if k == 2:
                        v.tensor_tensor(inv[:, q, :], dinv_all[:, cols], dinv_all[:, cols], ALU.mult)
                    dve.wait_ge(own_ld[p], 16 * (i - GS + 1))
                    if k == 3:
                        v.tensor_tensor(al[:, q, :, 0:2], own[:, p, :, D:R],
                                        deg_all[:, cols].rearrange("p (u a) -> p u a", a=1).broadcast_to([P, 2, 2]),
                                        ALU.mult)
                        v.tensor_tensor(al[:, q, :, 2], dinv_all[:, cols], deg_all[:, cols], ALU.mult)
                for u in range(2):
                    if u == 1 and (kd["first"][1] or not kd["edge"][1]):
                        dve.wait_ge(ps_ready, 2 * s + 8 + 2)
                    else:
                        dve.wait_ge(carry_ready, 2 * s + 2 + u)
                    ps = pse[2 * q + u][:, 0:D + 1]
                    if k == 1:
                        last = v.scalar_tensor_tensor(t1[:, q, u, 0:D + 1], hd[:, p, u, 0:D + 1],
                                                      rs[:, q, 10 + u:11 + u], ps, ALU.mult, ALU.add)
                    else:
                        last = v.tensor_tensor(t1[:, q, u, 0:D + 1], ps, own[:, p, u, 0:D + 1], ALU.add)
                last.then_inc(t1_ready, 1)
            walk(dve, step)

            dve.wait_ge(s_inside, 1)
            n_inside = dve.value_load(inside[0:1, 0:1], min_val=0, max_val=E)
            with dve.If(n_inside > 0):
                for p in range(SLOTS):
                    dve.wait_ge(out_sc[p], 32 * GS)
                v.memset(osb[:, 0, 0:2, :], 0.0).then_inc(zero_ready, 1)
                with dve.Fori(0, HT) as t:
                    dve.wait_ge(key_ld, 16 * t + 16)
                    v.scalar_tensor_tensor(same_key[:, :], key_row[:, :], key[:, bass.ds(t, 1)], scanmat[:, 0:P],
                                           ALU.is_equal, ALU.mult).then_inc(same_ready, 1)
                    dve.wait_ge(same_ready, t + 1)
                    v.tensor_reduce(later[:, :], same_key[:, :], mybir.AxisListType.X, ALU.max).then_inc(later_ready, 1)
                    dve.wait_ge(later_ready, t + 1)
                    v.scalar_tensor_tensor(cell[:, bass.ds(t, 1)], later[:, :], BIG, key[:, bass.ds(t, 1)],
                                           ALU.mult, ALU.add).then_inc(cell_ready, 1)
                dve.wait_ge(zero_st, 16)
                with dve.Fori(0, DENSE) as t:
                    dve.wait_ge(l_x, 16 * t + 16)
                    for j in range(4):
                        last = v.bn_stats(st[:, j, :], xin[:, 0, j, :])
                    named(last, l_stats, t)
                    v.tensor_tensor(diff[:, 0:4], st[:, 0:4, 1], st[:, 0:4, 4], ALU.subtract)
                    named(v.tensor_tensor(both[:, 0:4, :], st[:, 0:4, 1:3], st[:, 0:4, 4:6], ALU.add), l_sums, t)
                    v.tensor_tensor(square[:, 0:4], diff[:, 0:4], diff[:, 0:4], ALU.mult)
                    named(v.tensor_scalar(scaled[:, 0:4], both[:, 0:4, 1], 1.0 / D, EPS, ALU.mult, ALU.add), l_squares, t)
                    v.scalar_tensor_tensor(vv[:, 0:4], square[:, 0:4], 0.25, scaled[:, 0:4], ALU.mult, ALU.add)\
                        .then_inc(l_var, 1)
                    dve.wait_ge(l_sqrt, t + 1)
                    named(v.reciprocal(y[:, 0:4], sq[:, 0, 0:4]), l_rs[0], t)
                    named(v.scalar_tensor_tensor(yy[:, 0:4], y[:, 0:4], -0.5, y[:, 0:4], ALU.mult, ALU.mult), l_rs[1], t)
                    named(v.tensor_tensor(yyv[:, 0:4], yy[:, 0:4], vv[:, 0:4], ALU.mult), l_rs[2], t)
                    named(v.scalar_tensor_tensor(rs[:, 0, 0:4], yyv[:, 0:4], 1.5, y[:, 0:4], ALU.add, ALU.mult), l_rs[3], t)
                    v.scalar_tensor_tensor(nb[:, 0, 0:4], both[:, 0:4, 0], -0.5, rs[:, 0, 0:4], ALU.mult, ALU.mult)\
                        .then_inc(l_nb, 1)
                    dve.wait_ge(l_mm, t + 1)
                    for k in range(2):
                        last = v.tensor_tensor(osb[:, 0, 2 * k:2 * k + 2, :], mm[k][:, :].rearrange("p (j d) -> p j d", j=2),
                                               xin[:, 0, 2 * k:2 * k + 2, :], ALU.add)
                    last.then_inc(l_add, 1)

        @block.scalar
        def _(act):
            a = nc.scalar
            act.sem_inc(norm_done, 4)

            def copy_row(frm, to):
                a.activation(to, frm, ACT.Copy).then_inc(carry_ready, 1)

            def update(s, i, p, q, k):
                if k == 1:
                    wait_past(act, v_st[1][p], 16 * i)
                else:
                    act.wait_ge(v_st[1][p], 16 * GS)
                    wait_past(act, v_st[2][p], 16 * (i - GS))
                act.wait_ge(t1_ready, s + 1 + 4)
                if k == 2:
                    a.activation(vout[:, p, :, D + 1:R], own[:, p, :, D:D + 1], ACT.Copy)
                for u in range(2):
                    last = a.activation(vout[:, p, u, 0:D + 1], t1[:, q, u, 0:D + 1], ACT.Copy,
                                        scale=inv[:, q, u:u + 1])
                last.then_inc(vout_ready, 1)

            def evac(s, k):
                act.wait_ge(tp_ready, 2 * s + k + 1 + 4)
                wait_past(act, mm_ready, 2 * s + k - 1)
                a.activation(hT[:, k, :], tp[k][:, :], ACT.Relu).then_inc(hT_ready, 1)

            def step(s, i, p, kd):
                q = p % 2
                (i1, p1), (i2, p2) = back(i, p, 1), back(i, p, 2)
                k, k1, k2 = kd["edge"][0:3]
                hi = 12 if k2 == 1 else 10 if k == 1 else 4 if kd["dense"][0] else 0
                if hi:
                    act.wait_ge(var_ready, s + 1)
                    a.activation(sq[:, q, 0:hi], vv[:, 0:hi], ACT.Sqrt).then_inc(sqrt_ready, 1)
                if k == 1:
                    act.dma_start(own_x[bass.ds(2 * P * s, 2 * P), :].rearrange("(u p) r -> p u r", p=P),
                                  xe[:, p, 2:4, :]).then_inc(ox_st[p], 16)
                if kd["first"][1]:
                    wait_past(act, carry_ready, 2 * (s - 1))
                    act.sem_inc(carry_ready, 1)
                    if k2:
                        update(s - 2, i2, p2, q, k2)
                if k1 and not kd["first"][1]:
                    if k1 > 1:
                        act.wait_ge(v_ld[p1], 32 * (i1 - GS + 1))
                    else:
                        act.wait_ge(norm_done, s + 4)
                    act.wait_ge(ps_ready, 2 * (s - 2) + 8 + 2)
                    copy_row(pse[2 * q + 1][0:1, 0:R], msg[0:1, p1, 0, :])
                if kd["dense"][1]:
                    evac(s - 1, 0)
                if k1:
                    if kd["first"][1] and k1 > 1:
                        act.wait_ge(v_ld[p1], 32 * (i1 - GS + 1))
                    if kd["first"][1] and k1 == 1:
                        act.wait_ge(norm_done, s + 4)
                    act.wait_ge(ps_ready, 2 * (s - 1) + 8 + 1)
                    copy_row(pse[2 * (p1 % 2)][0:1, 0:R], msg[0:1, p1, 1, :])
                if k2 == 3:
                    act.wait_ge(ttp_ready, in_pass(s - 2, 3) + 1)
                    wait_past(act, fin_mm, in_pass(s - 2, 3))
                    a.activation(aT[0:3, :], tp[1][0:3, 0:2 * P], ACT.Copy)
                    a.activation(tT[:, :], tp[0][:, :], ACT.Copy).then_inc(tT_ready, 1)
                if kd["dense"][1]:
                    evac(s - 1, 1)
                if kd["dense"][0]:
                    act.wait_ge(tp_ready, 2 * s + 2)
                    act.wait_ge(nb_ready, s + 1)
                    for j in range(4):
                        last = a.activation(xn[:, q, j, :], xin[:, p, j, :], ACT.Relu, scale=rs[:, q, j:j + 1],
                                            bias=nb[:, q, j:j + 1])
                    last.then_inc(xn_ready, 1)
                if k == 1:
                    wait_past(act, plain_st[p], 16 * i)
                    act.wait_ge(t1_ready, s + 1)
                    act.wait_ge(nb_ready, s + 1)
                    for j in range(4):
                        to = msg[:, p, j, 0:D] if j < 2 else hd[:, p, j - 2, 0:D]
                        a.activation(to, xe[:, p, j, :], ACT.Relu, scale=rs[:, q, 4 + j:5 + j], bias=nb[:, q, 4 + j:5 + j])
                    a.activation(msg[:, p, :, D], rs[:, q, 8:10], ACT.Copy).then_inc(norm_done, 1)
                if k2 in (1, 2) and not kd["first"][1]:
                    update(s - 2, i2, p2, q, k2)
            walk(act, step)

            act.wait_ge(s_inside, 1)
            n_inside = act.value_load(inside[0:1, 0:1], min_val=0, max_val=E)
            with act.If(n_inside > 0):
                with act.Fori(0, DENSE) as t:
                    act.wait_ge(l_var, t + 1)
                    a.activation(sq[:, 0, 0:4], vv[:, 0:4], ACT.Sqrt).then_inc(l_sqrt, 1)
                    act.wait_ge(l_nb, t + 1)
                    for j in range(4):
                        last = a.activation(xn[:, 0, j, :], xin[:, 0, j, :], ACT.Relu, scale=rs[:, 0, j:j + 1],
                                            bias=nb[:, 0, j:j + 1])
                    last.then_inc(l_xn, 1)
                    act.wait_ge(l_tp, t + 1)
                    for k in range(2):
                        last = a.activation(hT[:, k, :], tp[k][:, :], ACT.Copy)
                    last.then_inc(l_hT, 1)

        @block.tensor
        def _(pe):
            t = nc.tensor
            pe.sem_inc(ps_ready, 8)
            pe.sem_inc(tp_ready, 4)
            pe.sem_inc(oh_used, 4)
            pe.wait_ge(s_const, 3)
            pe.wait_ge(s_w, 6 * 16)
            for w, b in ((W[1], 0), (W[0], 1)):
                for kc in range(DC):
                    for mc in range(DC):
                        o = (kc * DC + mc) * P
                        last = t.transpose(bank[b][:, o:o + P], w[:, mc, kc * P:(kc + 1) * P], ident[:, :])
            last.then_inc(s_pre, 1)

            def product(b, lhsT, rhs, wide):
                for mc in range(DC):
                    for kc in range(DC):
                        last = t.matmul(bank[b][:, mc * D:(mc + 1) * D], lhsT[:, kc, mc * P:(mc + 1) * P], rhs[:, kc, :],
                                        start=kc == 0, stop=kc == DC - 1)
                return last
            def histogram(i, j, start, stop):
                pe.wait_ge(oh_ready, 4 * i + j + 1)
                half = HI // 2
                t.matmul(bank[5][:, 0:half], olo[:, j, :], ohi[:, j, 0:half], start=start, stop=stop)
                t.matmul(bank[6][:, 0:half], olo[:, j, :], ohi[:, j, half:HI], start=start, stop=stop)\
                    .then_inc(oh_used, 1)
            for j in range(SLOTS):
                histogram(0, j, j == 0, False)
            with pe.Fori(1, HT // SLOTS - 1) as i:
                for j in range(SLOTS):
                    histogram(i, j, False, False)
            for j in range(SLOTS):
                histogram(HT // SLOTS - 1, j, False, j == SLOTS - 1)
            pe.wait_ge(s_wt, 1)
            product(2, WT[1], W[2], D).then_inc(s_pre, 1)
            pe.wait_ge(s_wt, 2)
            product(3, WT[0], W23, D)
            for k, (o, w) in enumerate(((0, W23), (D, W[2]))):
                for kc in range(DC):
                    last = t.matmul(bank[4][0:1, o:o + D], bcol[:, k, kc:kc + 1], w[:, kc, :],
                                    start=kc == 0, stop=kc == DC - 1)
            last.then_inc(s_pre, 1)
            pe.wait_ge(s_hist, 1)
            pe.wait_ge(s_beta, 1)
            for c in range(HC):
                last = t.matmul(bank[c][:, 0:2 * P + 1], hist[:, c * P:(c + 1) * P], scanmat[:, :], start=True, stop=True)
            last.then_inc(s_pre, 1)
            pe.wait_ge(s_tot, 1)
            t.matmul(bank[7][:, 0:HC], scanmat[:, 0:P], rowtot[:, :], start=True, stop=True)
            t.matmul(bank[7][:, 8:8 + HC], ones[:, :], rowtot[:, :], start=True, stop=True)
            t.matmul(bank[7][:, 16:17], ones[:, :], few[:, :], start=True, stop=True).then_inc(s_pre, 1)
            pe.wait_ge(s_tab, 1)
            pe.wait_ge(s_rows, 9 * 16)

            def transposes(s, q, k):
                pe.wait_ge(xn_ready, s + 1)
                wait_past(pe, hT_ready, 2 * s + k - 1)
                for j in range(2):
                    for c in range(DC):
                        o = (j * DC + c) * P
                        last = t.transpose(tp[k][:, o:o + P], xn[:, q, 2 * k + j, c * P:(c + 1) * P], ident[:, :])
                last.then_inc(tp_ready, 1)

            def dense(s, k):
                pe.wait_ge(hT_ready, 2 * s + k + 1)
                pe.wait_ge(mm_used, 2 * s + 7 + k)
                t.matmul(mm[k][:, :], ones_b[:, :], bias_rhs[:, :], start=True, stop=False)
                for j in range(2):
                    for c in range(DC):
                        o = (j * DC + c) * P
                        last = t.matmul(mm[k][:, j * D:(j + 1) * D], hT[:, k, o:o + P], W123[:, c, :],
                                        start=False, stop=j == 1 and c == DC - 1)
                last.then_inc(mm_ready, 1)

            def sums(s, i, p, k, first, u):
                q = p % 2
                pe.wait_ge(S_ready, s + 4 + 1)
                if first and u == 0:
                    if k == 1:
                        pe.wait_ge(norm_done, s + 4 + 1)
                    else:
                        pe.wait_ge(v_ld[p], 32 * (i - GS + 1))
                pe.wait_ge(carry_ready, 2 * s + 1 + u)
                pe.wait_ge(t1_ready, s + 3)
                t.matmul(pse[2 * q + u][:, 0:R], S[:, q, u, :], msg[:, p, u, :], start=True, stop=True)\
                    .then_inc(ps_ready, 1)

            def step(s, i, p, kd):
                q = p % 2
                i1, p1 = back(i, p, 1)
                k1, k2 = kd["edge"][1], kd["edge"][2]
                if kd["dense"][1]:
                    transposes(s - 1, p1 % 2, 0)
                if kd["dense"][2]:
                    dense(s - 2, 1)
                if k1:
                    sums(s - 1, i1, p1, k1, kd["first"][1], 0)
                if k2 == 3:
                    pe.wait_ge(t1_ready, s - 2 + 4 + 1)
                    wait_past(pe, tT_ready, in_pass(s - 2, 3))
                    for u in range(2):
                        t.transpose(tp[1][0:3, u * P:(u + 1) * P], al[:, q, u, 0:3], ident[:, :])
                        for c in range(DC):
                            o = (u * DC + c) * P
                            last = t.transpose(tp[0][:, o:o + P], t1[:, q, u, c * P:(c + 1) * P], ident[:, :])
                    last.then_inc(ttp_ready, 1)
                if kd["dense"][1]:
                    transposes(s - 1, p1 % 2, 1)
                    dense(s - 1, 0)
                if k1:
                    sums(s - 1, i1, p1, k1, kd["first"][1], 1)
                if k2 == 3:
                    pe.wait_ge(tT_ready, in_pass(s - 2, 3) + 1)
                    pe.wait_ge(fin_ready, in_pass(s - 4, 3) + 1 + 4)
                    for u in range(2):
                        for c in range(DC):
                            o = (u * DC + c) * P
                            t.matmul(mm[q][:, u * D:(u + 1) * D], tT[:, o:o + P], W123[:, c, :], start=c == 0, stop=False)
                        last = t.matmul(mm[q][:, u * D:(u + 1) * D], aT[:, u * P:(u + 1) * P], beta3[:, :],
                                        start=False, stop=True)
                    last.then_inc(fin_mm, 1)
            walk(pe, step)

            pe.wait_ge(s_inside, 1)
            n_inside = pe.value_load(inside[0:1, 0:1], min_val=0, max_val=E)
            with pe.If(n_inside > 0):
                pe.wait_ge(wm_ld, 16)
                with pe.Fori(0, DENSE) as n:
                    pe.wait_ge(l_xn, n + 1)
                    for k in range(2):
                        for j in range(2):
                            for c in range(DC):
                                o = (j * DC + c) * P
                                last = t.transpose(tp[k][:, o:o + P], xn[:, 0, 2 * k + j, c * P:(c + 1) * P], ident[:, :])
                    last.then_inc(l_tp, 1)
                    pe.wait_ge(l_hT, n + 1)
                    for k in range(2):
                        for j in range(2):
                            for c in range(DC):
                                o = (j * DC + c) * P
                                last = t.matmul(mm[k][:, j * D:(j + 1) * D], hT[:, k, o:o + P], Wm[:, c, :],
                                                start=c == 0, stop=c == DC - 1)
                    last.then_inc(l_mm, 1)


def kernel(**inputs):
    import numpy as np
    import concourse.bacc as bacc
    from concourse.bass_utils import run_bass_kernel_spmd

    x = np.asarray(inputs["x"])
    src, dst, weight = (np.asarray(inputs[n]) for n in ("src", "dst", "edge_weight"))
    xp = np.zeros((NP_, D), x.dtype)
    xp[:N] = x
    d = np.full(TILES * PER + 2, N, np.int32)
    d[0], d[1:E + 1], d[-1] = -1, dst, N + 2
    sr = np.full(TILES * PER + 2, N + 1, np.int32)
    sr[1:E + 1] = src
    tile = np.arange(TILES)[::-1, None] * PER + 1
    lane = np.arange(1, P)[None, :] - 1

    def tiles(first, others):
        return np.concatenate([first, others], axis=1)

    own = tiles(d[tile], d[tile + lane])
    prev = tiles(d[tile], d[tile + lane - 1])
    col = tiles(d[tile + PER], d[tile + lane])
    srcs = tiles(np.full((TILES, 1), N + 1, np.int32), sr[tile + lane])

    def by_tiles(a, fill):
        return np.ascontiguousarray(np.concatenate([a, np.full(HT * P - E, fill, a.dtype)]).reshape(HT, P).T)

    def steps(a):
        return a.reshape(STEPS, 2, P).transpose(2, 0, 1)

    arrays = {
        "x": xp,
        "idx_ends": np.ascontiguousarray(np.concatenate([steps(srcs), steps(own)], axis=2)),
        "prev_ends": np.ascontiguousarray(steps(prev)),
        "col_ends": np.ascontiguousarray(col.T),
        "row_ends": np.ascontiguousarray(own.reshape(1, TILES * P)),
        "dst_nat": by_tiles(dst, N),
        "src_nat": by_tiles(src, N),
        "weight_nat": by_tiles(weight, 0),
    }
    for n in ("W1", "b1", "W2", "b2", "W3", "b3"):
        a = np.asarray(inputs["L0_gnn_" + n])
        arrays[n] = np.ascontiguousarray(a.reshape(DC, P).T if n in ("b1", "b2") else a)
    nc = bacc.Bacc("TRN2", target_bir_lowering=False, num_devices=1)
    args = [nc.dram_tensor("in_" + n, a.shape, mybir.dt.from_np(a.dtype), kind="ExternalInput").ap()
            for n, a in arrays.items()]
    out = nc.dram_tensor("out", (NP_, D), F32, kind="ExternalOutput").ap()
    gnn(nc, *args, out)
    r = run_bass_kernel_spmd(nc, [{"in_" + n: a for n, a in arrays.items()}], core_ids=[0])
    return r.results[0]["out"][:N]
```

```python
import concourse.bass as bass
from concourse import mybir
from contextlib import ExitStack

F32 = mybir.dt.float32
F16 = mybir.dt.float16
BF16 = mybir.dt.bfloat16
I32 = mybir.dt.int32
ALU = mybir.AluOpType
ACT = mybir.ActivationFunctionType

P = 128
N = 100000
D = 256
DC = D // P
E = 25000
EPS = 1e-5
ROWS = 512
DENSE = (N + ROWS - 1) // ROWS
NP_ = DENSE * ROWS
HI = NP_ // P
HC = (HI + P - 1) // P
HALF = HI // 2
PER = P - 1
TILES = 200
STEPS = TILES // 2
HT = (E + P - 1) // P
R = D + 2
T = TILES * P
SLOTS = 4
RING = 14
BIG = float(1 << 20)
MAGIC = 1.5 * (1 << 23)
assert HT % RING == 0 and STEPS % SLOTS == 0 and TILES * PER >= E and 2 * STEPS > DENSE and DENSE % SLOTS == 0


def gnn(nc, x, idx_ends, prev_ends, col_ends, row_ends, dst_nat, src_nat, weight_nat, W1, b1, W2, b2, W3, b3, out):
    ctx = ExitStack()
    with ctx:
        def sb(name, shape, dt=F32):
            return ctx.enter_context(nc.sbuf_tensor(name, shape, dt))

        def sem(name):
            return ctx.enter_context(nc.semaphore(name))

        def sems(name, n):
            return [sem(f"{name}{i}") for i in range(n)]

        node_table = nc.dram_tensor("node_table", (NP_, 2), F32).ap()
        own_x = nc.dram_tensor("own_x", (TILES * P, D), F32).ap()
        cells = nc.dram_tensor("cells", (D * D, 1), F32).ap()
        key_rows = nc.dram_tensor("key_rows", (HT, P), F32).ap()
        states = nc.dram_tensor("states", (3 * T, R), F32).ap()
        V = [None, states[0:T, :], states[2 * T:3 * T, :]]
        plain = states[T:2 * T, :]

        ident = sb("ident", [P, P])
        scanmat = sb("scanmat", [P, 2 * P + 1])
        ones = sb("ones", [P, P])
        iota = sb("iota", [P, HALF], F16)
        W = [sb(f"W{k}", [P, DC, D]) for k in (1, 2, 3)]
        WT = [sb(f"WT{k}", [P, DC, D]) for k in (1, 2)]
        W23 = sb("W23", [P, DC, D])
        W123 = sb("W123", [P, DC, D])
        bcol = sb("bcol", [P, 2, DC])
        beta = sb("beta", [1, 3, D])
        beta3 = sb("beta3", [P, D])
        bsum = sb("bsum", [1, 4, D])
        bparts = sb("bparts", [1, 3, D], BF16)
        bias_rhs = sb("bias_rhs", [P, 2 * D], BF16)
        ones_b = sb("ones_b", [P, P], BF16)
        dnat = sb("dnat", [P, HT], I32)
        hilo = sb("hilo", [P, 2, HT], I32)
        hilof = sb("hilof", [P, 2, HT])
        ohi = sb("ohi", [P, RING, HALF], F16)
        olo = sb("olo", [P, RING, 2 * P], F16)
        hist = sb("hist", [P, HC * P])
        rowtot = sb("rowtot", [P, HC])
        base = sb("base", [P, 2, HC])
        tab = sb("tab", [P, HC, P, 2])
        lb = sb("lb", [P, HC, P])
        ta = sb("ta", [P, HC, P])
        snat = sb("snat", [P, HT], I32)
        pair = sb("pair", [P, 3, HT])
        few = sb("few", [P, 1])
        inside = sb("inside", [P, 1], I32)
        key = sb("key", [P, HT])
        key_row = sb("key_row", [P, P])
        same_key = sb("same_key", [P, P])
        later = sb("later", [P, 1])
        cell = sb("cell", [P, HT], I32)
        cell_col = sb("cell_col", [P, 1], I32)
        weights = sb("weights", [P, HT])
        weight_col = sb("weight_col", [P, 1])
        Wm = sb("Wm", [P, DC, D])
        idx_ends_sb = sb("idx_ends_sb", [P, STEPS, 4], I32)
        idx_slots = sb("idx_slots", [P, STEPS, 2], I32)
        idx_slots3 = sb("idx_slots3", [P, STEPS, 2], I32)
        idx_out = sb("idx_out", [P, STEPS, 2], I32)
        plain_rows = sb("plain_rows", [P, STEPS, 2])
        prev_sb = sb("prev_sb", [P, STEPS, 2], I32)
        col_sb = sb("col_sb", [P, TILES], I32)
        rep = sb("rep", [P, 3, STEPS, 2])
        shift = sb("shift", [P, STEPS, 2])
        dinv_all = sb("dinv_all", [P, TILES])
        root_all = sb("root_all", [P, TILES])
        deg_all = sb("deg_all", [P, TILES])
        xin = sb("xin", [P, SLOTS, 4, D])
        osb = sb("osb", [P, SLOTS, 4, D])
        xn = sb("xn", [P, 2, 4, D])
        hT = sb("hT", [P, 2, 2, 2 * DC * P])
        st = sb("st", [P, 8, 6])
        diff = sb("diff", [P, 8])
        both = sb("both", [P, 8, 2])
        square = sb("square", [P, 8])
        scaled = sb("scaled", [P, 8])
        vv = sb("vv", [P, 12])
        sq = sb("sq", [P, 2, 12])
        y = sb("y", [P, 12])
        yy = sb("yy", [P, 12])
        yyv = sb("yyv", [P, 12])
        rs = sb("rs", [P, 2, 12])
        nb = sb("nb", [P, 2, 8])
        inv = sb("inv", [P, 2, 2])
        sidx = sb("sidx", [P, SLOTS, 8], I32)
        xe = sb("xe", [P, SLOTS, 4, D])
        tg = sb("tg", [P, SLOTS, 2, 2])
        msg = sb("msg", [P, SLOTS, 2, R])
        hd = sb("hd", [P, SLOTS, 2, R])
        drow = sb("drow", [P, SLOTS, 2 * P], I32)
        S = sb("S", [P, SLOTS, 2, P])
        own = sb("own", [P, SLOTS, 2, R])
        t1 = sb("t1", [P, 2, 2, R])
        vout = sb("vout", [P, SLOTS, 2, R])
        al = sb("al", [P, 2, 2, 4])
        tT = sb("tT", [P, 2 * DC * P])
        aT = sb("aT", [P, 2 * P])
        scat = sb("scat", [P, SLOTS, 2], I32)

        bank = [ctx.enter_context(nc.psum_tensor(f"bank{i}", [P, 512], F32)) for i in range(8)]
        tp, mm, pse = bank[0:2], bank[2:4], bank[4:8]

        s_idx = sem("s_idx")
        s_w = sem("s_w")
        s_const = sem("s_const")
        s_mem = sem("s_mem")
        sp_turn = sem("sp_turn")
        s_dnat = sem("s_dnat")
        s_rows = sem("s_rows")
        s_table = sem("s_table")
        x_ld = sems("x_ld", SLOTS)
        o_st = sems("o_st", SLOTS)
        drow_ld = sems("drow_ld", SLOTS)
        own_ld = sems("own_ld", SLOTS)
        plain_st = sems("plain_st", SLOTS)
        ox_st = sems("ox_st", SLOTS)
        v_st = [None, sems("v1_st", SLOTS), sems("v2_st", SLOTS)]
        xe_ld = sems("xe_ld", SLOTS)
        tg_ld = sems("tg_ld", SLOTS)
        v_ld = sems("v_ld", SLOTS)
        xd_ld = sems("xd_ld", SLOTS)
        out_sc = sems("out_sc", SLOTS)
        s_set = sem("s_set")
        s_pre = sem("s_pre")
        oh_ready = sem("oh_ready")
        oh_used = sem("oh_used")
        s_wt = sem("s_wt")
        s_banks = sem("s_banks")
        s_beta = sem("s_beta")
        s_hist = sem("s_hist")
        s_scan = sem("s_scan")
        s_tab = sem("s_tab")
        s_rep = sem("s_rep")
        sidx_ready = sem("sidx_ready")
        pool_turn = sem("pool_turn")
        stats_done = sem("stats_done")
        sums_done = sem("sums_done")
        squares_done = sem("squares_done")
        var_ready = sem("var_ready")
        sqrt_ready = sem("sqrt_ready")
        recip_done = sem("recip_done")
        recip2_done = sem("recip2_done")
        recip3_done = sem("recip3_done")
        diff_done = sem("diff_done")
        scaled_done = sem("scaled_done")
        rs_ready = sem("rs_ready")
        nb_ready = sem("nb_ready")
        scale_ready = sem("scale_ready")
        norm_done = sem("norm_done")
        xn_ready = sem("xn_ready")
        tp_ready = sem("tp_ready")
        hT_ready = sem("hT_ready")
        mm_ready = sem("mm_ready")
        mm_used = sem("mm_used")
        S_ready = sem("S_ready")
        carry_ready = sem("carry_ready")
        ps_ready = sem("ps_ready")
        t1_ready = sem("t1_ready")
        vout_ready = sem("vout_ready")
        tT1_ready = sem("tT1_ready")
        ttp_ready = sem("ttp_ready")
        tT0_ready = sem("tT0_ready")
        fin_mm = sem("fin_mm")
        root_ready = sem("root_ready")
        slots3_ready = sem("slots3_ready")
        fin_ready = sem("fin_ready")

        s_inside = sem("s_inside")
        keys_st = sem("keys_st")
        weights_ld = sem("weights_ld")
        zero_ready = sem("zero_ready")
        zero_st = sem("zero_st")
        key_ld = sem("key_ld")
        same_ready = sem("same_ready")
        later_ready = sem("later_ready")
        cell_ready = sem("cell_ready")
        cell_copied = sem("cell_copied")
        cell_st = sem("cell_st")
        wm_ld = sem("wm_ld")
        l_x = sem("l_x")
        l_stats = sem("l_stats")
        l_sums = sem("l_sums")
        l_squares = sem("l_squares")
        l_var = sem("l_var")
        l_sqrt = sem("l_sqrt")
        l_rs = sems("l_rs", 4)
        l_nb = sem("l_nb")
        l_xn = sem("l_xn")
        l_tp = sem("l_tp")
        l_hT = sem("l_hT")
        l_mm = sem("l_mm")
        l_add = sem("l_add")
        l_st = sem("l_st")

        block = ctx.enter_context(nc.Block())

        def edge_pass(s):
            return s // STEPS + 1 if 0 <= s < 3 * STEPS else 0

        def is_dense(s):
            return 0 <= s < DENSE

        def kinds(s):
            return {"edge": [edge_pass(s - l) for l in range(5)], "dense": [is_dense(s - l) for l in range(5)],
                    "first": [edge_pass(s - l) > 0 and (s - l) % STEPS == 0 for l in range(5)],
                    "begins": s // SLOTS % GS if s // SLOTS % GS < 2 else 2}

        def walk(eng, step):
            groups, g = (3 * STEPS + SLOTS) // SLOTS, 0
            while g < groups:
                same = [kinds(SLOTS * g + p) for p in range(SLOTS)]
                e = g + 1
                while e < groups and [kinds(SLOTS * e + p) for p in range(SLOTS)] == same:
                    e += 1
                if e - g == 1:
                    for p in range(SLOTS):
                        step(SLOTS * g + p, g, p, same[p])
                else:
                    with eng.Fori(g, e) as i:
                        for p in range(SLOTS):
                            step(SLOTS * i + p, i, p, same[p])
                g = e

        def back(i, p, lag):
            return (i if p >= lag else i - 1), (p - lag) % SLOTS

        def wait_past(eng, semaphore, value):
            if not isinstance(value, int) or value > 0:
                eng.wait_ge(semaphore, value)

        GS = STEPS // SLOTS

        def in_pass(s, k):
            return s - (k - 1) * STEPS

        @block.sync
        def _(sp):
            sp.dma_start(dnat[:, :], dst_nat).then_inc(s_dnat, 16)
            for tile, dram in ((idx_ends_sb, idx_ends), (prev_sb, prev_ends)):
                sp.dma_start(tile[:, :, :], dram).then_inc(s_idx, 16)
            sp.dma_start(snat[:, :], src_nat).then_inc(s_idx, 16)
            sp.dma_start(col_sb[:, :], col_ends).then_inc(s_idx, 16)
            for tile, dram in zip(W, (W1, W2, W3)):
                sp.dma_start(tile[:, :, :], dram.rearrange("(c p) n -> p c n", p=P)).then_inc(s_w, 16)
            for k, b in enumerate((b1, b2)):
                sp.dma_start(bcol[:, k, :], b).then_inc(s_w, 16)
            sp.dma_start(beta[0:1, 2, :], b3.rearrange("(a n) -> a n", a=1)).then_inc(s_w, 16)

            sp.wait_ge(s_tab, 1)
            full = HI // P
            sp.dma_start(node_table[0:full * P * P, :].rearrange("(c p l) k -> p c (l k)", p=P, l=P),
                         tab[:, 0:full, :, :].rearrange("p c l k -> p c (l k)")).then_inc(s_table, 16)
            sp.dma_start(node_table[full * P * P:NP_, :].rearrange("(p l) k -> p (l k)", l=P),
                         tab[0:HI - full * P, full, :, :].rearrange("p l k -> p (l k)")).then_inc(s_table, 16)

            def wait(semaphore, value):
                sp.wait_ge(semaphore, value)
                sp.sem_inc(sp_turn, 1)

            def load_front(s, p, kd):
                row, slot_free = ROWS * s, 2 * s + 2
                k = kd["edge"][0]
                if k:
                    s1, edge_row = s + 1, 2 * P * in_pass(s, k)
                if kd["dense"][0]:
                    wait(mm_used, slot_free)
                    sp.dma_start(xin[:, p, :, :], x[bass.ds(row, ROWS), :].rearrange("(p j) d -> p j d", j=4))\
                        .then_inc(x_ld[p], 16)
                if k:
                    wait(S_ready, s1)
                    sp.dma_start(drow[:, p, :], row_ends[:, bass.ds(edge_row, 2 * P)].broadcast_to([P, 2 * P]))\
                        .then_inc(drow_ld[p], 16)

            def load_own(s, i, p, k):
                s1, rows = s + 1, bass.ds(2 * P * in_pass(s, k), 2 * P)
                stored = 16 * (i - (k - 1) * GS + 1)
                vout_read = s - 3 if k == 2 else 2 * STEPS - 4 + p + 1
                wait(v_st[k - 1][p], stored)
                wait(t1_ready, s1)
                wait(vout_ready, vout_read)
                sp.dma_start(own[:, p, :, :], V[k - 1][rows, :].rearrange("(u p) r -> p u r", p=P))\
                    .then_inc(own_ld[p], 16)

            def load_own_x(s, p):
                free, rows = in_pass(s, 3) + 1, bass.ds(2 * P * in_pass(s, 3), 2 * P)
                wait(ox_st[p], 16 * GS)
                wait(fin_ready, free)
                sp.dma_start(xe[:, p, 2:4, :], own_x[rows, :].rearrange("(u p) r -> p u r", p=P))\
                    .then_inc(xd_ld[p], 16)

            def store(s, p, k, dense):
                row, passed = ROWS * s, 2 * s + 8 + 2
                if k in (1, 2):
                    edge_row, updated = 2 * P * in_pass(s, k), s + 1
                    rows = bass.ds(edge_row, 2 * P)
                    wait(vout_ready, updated)
                    sp.dma_start(V[k][rows, :].rearrange("(u p) r -> p u r", p=P), vout[:, p, :, :])\
                        .then_inc(v_st[k][p], 16)
                    if k == 1:
                        wait(ps_ready, passed)
                        sp.dma_start(plain[rows, :].rearrange("(u p) r -> p u r", p=P), msg[:, p, :, :])\
                            .then_inc(plain_st[p], 16)
                if dense:
                    wait(mm_used, passed)
                    sp.dma_start(out[bass.ds(row, ROWS), :].rearrange("(p j) d -> p j d", j=4), osb[:, p, :, :])\
                        .then_inc(o_st[p], 16)

            def step(s, i, p, kd):
                k, k4 = kd["edge"][0], kd["edge"][4]
                load_front(s, p, kd)
                store(s - 4, p, k4, kd["dense"][4])
                if k > 1:
                    load_own(s, i, p, k)
                if kd["edge"][2] == 3:
                    load_own_x(s - 2, back(i, p, 2)[1])
            walk(sp, step)
            for p in range(SLOTS):
                sp.wait_ge(o_st[p], 16 * (DENSE // SLOTS))
                sp.wait_ge(out_sc[p], 32 * GS)

            sp.wait_ge(s_inside, 1)
            n_inside = sp.value_load(inside[0:1, 0:1], min_val=0, max_val=E)
            with sp.If(n_inside > 0):
                sp.dma_start(weights[:, :], weight_nat).then_inc(weights_ld, 16)
                sp.dma_start(key_rows.rearrange("t p -> p t"), key[:, :], allow_slow_non_contiguous=True)\
                    .then_inc(keys_st, 16)
                sp.wait_ge(zero_ready, 1)
                sp.dma_start(cells.rearrange("(p c) a -> p (c a)", p=P), osb[:, 0, 0:2, :].rearrange("p j d -> p (j d)"))\
                    .then_inc(zero_st, 16)
                sp.wait_ge(keys_st, 16)
                with sp.Fori(0, HT) as t:
                    seen = t + 1
                    sp.dma_start(key_row[:, :], key_rows[bass.ds(t, 1), :].broadcast_to([P, P])).then_inc(key_ld, 16)
                    wait(cell_ready, seen)
                sp.wait_ge(cell_st, 16 * HT)
                sp.dma_start(Wm[:, :, :], cells.rearrange("(c p n) a -> p c (n a)", p=P, n=D)).then_inc(wm_ld, 16)
                with sp.Fori(0, DENSE) as t:
                    row, added, stored = ROWS * t, t + 1, 16 * (t + 1)
                    rows = out[bass.ds(row, ROWS), :].rearrange("(p j) d -> p j d", j=4)
                    sp.dma_start(xin[:, 0, :, :], rows).then_inc(l_x, 16)
                    wait(l_add, added)
                    sp.dma_start(rows, osb[:, 0, :, :]).then_inc(l_st, 16)
                    wait(l_st, stored)

        @block.gpsimd
        def _(pool):
            pool.memset(ident[:, :], 0.0).then_inc(s_mem, 1)
            pool.memset(scanmat[:, 0:P], 1.0).then_inc(s_mem, 1)
            pool.memset(scanmat[:, P:2 * P], 0.0).then_inc(s_mem, 1)
            pool.memset(scanmat[:, 2 * P:2 * P + 1], 1.0).then_inc(s_mem, 1)
            pool.memset(ones[:, :], 1.0).then_inc(s_mem, 1)
            pool.memset(ones_b[:, :], 1.0).then_inc(s_mem, 1)
            pool.memset(bias_rhs[:, :], 0.0).then_inc(s_mem, 1)
            pool.memset(beta3[:, :], 0.0).then_inc(s_mem, 1)
            pool.memset(aT[:, :], 0.0).then_inc(s_mem, 1)
            pool.memset(hist[:, HI:HC * P], 0.0).then_inc(s_mem, 1)
            pool.memset(msg[:, :, :, D:R], 1.0).then_inc(s_mem, 1)
            pool.memset(hd[:, :, :, D:R], 1.0).then_inc(s_mem, 1)
            pool.memset(vout[:, :, :, D:R], 0.0).then_inc(s_mem, 1)
            pool.iota(iota[:, :], [[1, HALF]], base=0, channel_multiplier=0,
                      allow_small_or_imprecise_dtypes=True).then_inc(s_mem, 1)
            pool.iota(plain_rows[:, :, :], [[2 * P, STEPS], [P, 2]], base=T, channel_multiplier=1,
                      allow_small_or_imprecise_dtypes=True).then_inc(s_mem, 1)
            pool.wait_ge(s_mem, 15)
            for m in (ident[:, :], scanmat[:, P:2 * P]):
                pool.affine_select(out=m, in_=m, compare_op=ALU.not_equal, fill=1.0, base=0,
                                   pattern=[[-1, P]], channel_multiplier=1).then_inc(s_const, 1)
            pool.affine_select(out=scanmat[:, 0:P], in_=scanmat[:, 0:P], compare_op=ALU.is_gt, fill=0.0, base=0,
                               pattern=[[1, P]], channel_multiplier=-1).then_inc(s_const, 1)
            node_bound = pool.to_reg(NP_ - 1)
            pool.wait_ge(s_table, 32)
            pool.wait_ge(s_idx, 64)
            pool.wait_ge(s_rep, 1)

            def gather(to, table, index, ready, bound=None):
                pool.indirect_dma_start(out=to, out_offset=None, in_=table,
                                        in_offset=bass.IndirectOffsetOnAxis(ap=index, axis=0),
                                        bounds_check=bound, oob_is_err=False).then_inc(ready, 16)

            def step(s, i, p, kd):
                k = kd["edge"][0]
                if k:
                    col = pool.snap(in_pass(s, k)) if not isinstance(s, int) else in_pass(s, k)
                    if k == 1:
                        wait_past(pool, xe_ld[p], 64 * i)
                        wait_past(pool, tg_ld[p], 32 * i)
                    else:
                        pool.wait_ge(xe_ld[p], 64 * GS)
                        wait_past(pool, v_ld[p], 32 * (i - GS))
                    turn()
                    if k == 1:
                        pool.tensor_copy(sidx[:, p, 0:4], idx_ends_sb[:, bass.ds(col, 1), :]
                                         .rearrange("p a k -> p (a k)")).then_inc(sidx_ready, 1)
                    else:
                        pool.sem_inc(sidx_ready, 1)
                    if k != 1:
                        if k == 3 and kd["first"][0]:
                            pool.wait_ge(slots3_ready, 2)
                            turn()
                        pool.tensor_copy(sidx[:, p, 4:6], (idx_slots if k == 2 else idx_slots3)[:, bass.ds(col, 1), :]
                                         .rearrange("p a k -> p (a k)")).then_inc(sidx_ready, 1)
                    else:
                        pool.sem_inc(sidx_ready, 1)
                    pool.wait_ge(sidx_ready, 2 * s + 2)
                if k == 1:
                    pool.wait_ge(norm_done, s + 1)
                    wait_past(pool, ox_st[p], 16 * i)
                    turn()
                    for u in range(2):
                        gather(tg[:, p, u, :], node_table, sidx[:, p, u:u + 1], tg_ld[p])
                    for j in range(4):
                        gather(xe[:, p, j, :], x, sidx[:, p, j:j + 1], xe_ld[p])
                if k > 1:
                    if kd["first"][0]:
                        for q in range(SLOTS):
                            pool.wait_ge(v_st[k - 1][q], 16 * GS)
                            pool.wait_ge(plain_st[q], 16 * GS)
                    pool.wait_ge(ps_ready, 2 * s + 2)
                    turn()
                    for u in range(2):
                        gather(msg[:, p, u, :], states[0:2 * T, :] if k == 2 else states, sidx[:, p, 4 + u:5 + u], v_ld[p])
                if kd["edge"][4] == 3:
                    t = pool.snap(s - 4 - 2 * STEPS) if not isinstance(s, int) else s - 4 - 2 * STEPS
                    if kd["first"][4]:
                        for r in range(SLOTS):
                            pool.wait_ge(o_st[r], 16 * (DENSE // SLOTS))
                    pool.wait_ge(fin_ready, t + 1 + 4)
                    turn()
                    for u in range(2):
                        pool.indirect_dma_start(out=out,
                                                out_offset=bass.IndirectOffsetOnAxis(ap=scat[:, p, u:u + 1], axis=0),
                                                in_=osb[:, p, u, :], in_offset=None, bounds_check=node_bound,
                                                oob_is_err=False).then_inc(out_sc[p], 16)

            def turn():
                pool.sem_inc(pool_turn, 1)
            walk(pool, step)
            for p in range(SLOTS):
                pool.wait_ge(out_sc[p], 32 * GS)

            pool.wait_ge(s_inside, 1)
            n_inside = pool.value_load(inside[0:1, 0:1], min_val=0, max_val=E)
            with pool.If(n_inside > 0):
                cell_bound = pool.to_reg(D * D - 1)
                pool.wait_ge(weights_ld, 16)
                pool.wait_ge(zero_st, 16)
                pool.wait_ge(cell_ready, HT)
                turn()
                with pool.Fori(0, HT) as t:
                    pool.tensor_copy(cell_col[:, :], cell[:, bass.ds(t, 1)]).then_inc(cell_copied, 1)
                    pool.tensor_copy(weight_col[:, :], weights[:, bass.ds(t, 1)]).then_inc(cell_copied, 1)
                    pool.wait_ge(cell_copied, 2 * t + 2)
                    turn()
                    pool.indirect_dma_start(out=cells, out_offset=bass.IndirectOffsetOnAxis(ap=cell_col[:, 0:1], axis=0),
                                            in_=weight_col[:, 0:1], in_offset=None, bounds_check=cell_bound,
                                            oob_is_err=False).then_inc(cell_st, 16)
                    pool.wait_ge(cell_st, 16 * t + 16)
                    turn()

        @block.vector
        def _(dve):
            v = nc.vector
            count = [0]

            def link(ins):
                count[0] += 1
                ins.then_inc(s_set, 1)
                dve.wait_ge(s_set, count[0])

            dve.sem_inc(mm_used, 8)
            dve.sem_inc(S_ready, 4)
            dve.sem_inc(t1_ready, 4)
            dve.sem_inc(fin_ready, 4)

            dve.wait_ge(s_dnat, 16)
            v.tensor_scalar(hilo[:, 0, :], dnat[:, :], 8, None, ALU.logical_shift_right)
            link(v.tensor_scalar(hilo[:, 1, :], dnat[:, :], 2 * P - 1, None, ALU.bitwise_and))
            link(v.tensor_copy(hilof[:, :, :], hilo[:, :, :]))
            dve.wait_ge(s_const, 3)

            def onehots(i, j, c):
                dve.wait_ge(oh_used, RING * i + j + 1)
                v.tensor_scalar(ohi[:, j, :], iota[:, 0:HALF], hilof[:, 0, bass.ds(c, 1)], None, ALU.is_equal)
                v.tensor_scalar(olo[:, j, :], iota[:, 0:2 * P], hilof[:, 1, bass.ds(c, 1)], None, ALU.is_equal)\
                    .then_inc(oh_ready, 1)
            with dve.Fori(0, HT // RING) as i:
                for j in range(RING):
                    onehots(i, j, RING * i + j)

            dve.wait_ge(oh_used, RING + HT)
            v.tensor_copy(hist[:, 0:HI:2], bank[5][:, 0:HALF])
            v.tensor_copy(hist[:, 1:HI:2], bank[6][:, 0:HALF]).then_inc(s_hist, 1)
            dve.wait_ge(s_idx, 64)
            v.tensor_scalar(pair[:, 0, :], snat[:, :], D, None, ALU.min)
            link(v.tensor_scalar(pair[:, 1, :], dnat[:, :], D, None, ALU.min))
            link(v.tensor_tensor(pair[:, 2, :], pair[:, 0, :], pair[:, 1, :], ALU.max))
            link(v.scalar_tensor_tensor(pair[:, 0, :], pair[:, 0, :], float(D), pair[:, 1, :], ALU.mult, ALU.add))
            link(v.tensor_scalar(pair[:, 1, :], pair[:, 2, :], float(D), BIG, ALU.is_ge, ALU.mult))
            link(v.tensor_tensor(key[:, :], pair[:, 0, :], pair[:, 1, :], ALU.add))
            link(v.tensor_scalar(pair[:, 1, :], pair[:, 2, :], float(D), None, ALU.is_lt))
            link(v.tensor_reduce(few[:, :], pair[:, 1, :], mybir.AxisListType.X, ALU.add))
            ends = idx_ends_sb[:, :, 2:4]
            v.tensor_tensor(rep[:, 0, :, :], ends, prev_sb[:, :, :], ALU.not_equal)
            link(v.tensor_scalar(rep[:, 1, :, :], ends, -BIG, None, ALU.add))
            link(v.tensor_tensor(rep[:, 2, :, :], rep[:, 0, :, :], rep[:, 1, :, :], ALU.mult))
            v.tensor_scalar(idx_out[:, :, :], rep[:, 2, :, :], BIG, None, ALU.add).then_inc(s_rep, 1)
            for c in range(HC):
                dve.wait_ge(s_scan, c + 1)
                v.tensor_copy(rowtot[:, c:c + 1], bank[c][:, 2 * P:2 * P + 1])
                v.tensor_copy(lb[:, c, :], bank[c][:, 0:P])
                ins = v.tensor_copy(tab[:, c, :, 0], bank[c][:, P:2 * P])
            link(ins)
            dve.sem_inc(s_banks, 1)
            dve.wait_ge(s_pre, 2)
            v.tensor_copy(base[:, 0, :], bank[7][:, 0:HC])
            v.tensor_copy(inside[:, :], bank[7][:, 16:17]).then_inc(s_inside, 1)
            link(v.tensor_copy(base[:, 1, :], bank[7][:, 8:8 + HC]))
            for c in range(1, HC):
                link(v.tensor_scalar(base[:, 0, c:HC], base[:, 0, c:HC], base[:, 1, c - 1:c], None, ALU.add))
            link(v.tensor_tensor(lb[:, :, :], lb[:, :, :],
                                 base[:, 0, :].rearrange("p (c a) -> p c a", a=1).broadcast_to([P, HC, P]), ALU.add))
            link(v.tensor_scalar(ta[:, :, :], lb[:, :, :], 1.0 / PER, 0.5 / PER - 0.5, ALU.mult, ALU.add))
            link(v.tensor_scalar(ta[:, :, :], ta[:, :, :], MAGIC, -MAGIC, ALU.add, ALU.add))
            link(v.scalar_tensor_tensor(lb[:, :, :], ta[:, :, :], -float(P + PER), lb[:, :, :], ALU.mult, ALU.add))
            v.tensor_scalar(ta[:, :, :], tab[:, :, :, 0], 1.0, None, ALU.min)
            link(v.tensor_scalar(lb[:, :, :], lb[:, :, :], float((TILES - 1) * P + 1) - BIG, None, ALU.add))
            link(v.tensor_tensor(ta[:, :, :], ta[:, :, :], lb[:, :, :], ALU.mult))
            v.tensor_scalar(tab[:, :, :, 1], ta[:, :, :], BIG, None, ALU.add).then_inc(s_tab, 1)

            dve.wait_ge(s_wt, 3)
            link(v.tensor_tensor(bsum[0:1, 0, :], beta[0:1, 0, :], beta[0:1, 1, :], ALU.add))
            link(v.tensor_tensor(bsum[0:1, 1, :], bsum[0:1, 0, :], beta[0:1, 2, :], ALU.add))
            for k in range(2):
                link(v.tensor_copy(bparts[0:1, k, :], bsum[0:1, 1 + k, :]))
                link(v.tensor_tensor(bsum[0:1, 2 + k, :], bsum[0:1, 1 + k, :], bparts[0:1, k, :], ALU.subtract))
            v.tensor_copy(bparts[0:1, 2, :], bsum[0:1, 3, :]).then_inc(s_beta, 1)

            def named(ins, done, s):
                ins.then_inc(done, 1)
                dve.wait_ge(done, s + 1)

            def add(s, p, k):
                dve.wait_ge(mm_ready, 2 * s + k + 1)
                v.tensor_tensor(osb[:, p, 2 * k:2 * k + 2, :], mm[k][:, :].rearrange("p (j d) -> p j d", j=2),
                                xin[:, p, 2 * k:2 * k + 2, :], ALU.add).then_inc(mm_used, 1)

            def step(s, i, p, kd):
                q = p % 2
                (i1, p1), (i2, p2), (i3, p3) = (back(i, p, lag) for lag in (1, 2, 3))
                k, k2 = kd["edge"][0], kd["edge"][2]
                dense = kd["dense"][0]
                n = 8 if k == 1 else 4 if dense else 0
                hi = 12 if k2 == 1 else 10 if k == 1 else 4 if dense else 0
                if n:
                    dve.wait_ge(x_ld[p], 16 * (i + 1))
                    for j in range(4):
                        last = v.bn_stats(st[:, j, :], xin[:, p, j, :])
                    if k == 1:
                        dve.wait_ge(xe_ld[p], 64 * (i + 1))
                        for j in range(4):
                            last = v.bn_stats(st[:, 4 + j, :], xe[:, p, j, :])
                    named(last, stats_done, s)
                    v.tensor_tensor(diff[:, 0:n], st[:, 0:n, 1], st[:, 0:n, 4], ALU.subtract).then_inc(diff_done, 1)
                    v.tensor_tensor(both[:, 0:n, :], st[:, 0:n, 1:3], st[:, 0:n, 4:6], ALU.add).then_inc(sums_done, 1)
                if k == 1:
                    dve.wait_ge(tg_ld[p], 32 * (i + 1))
                    v.tensor_scalar(vv[:, 8:10], tg[:, p, :, 0], 1.0, None, ALU.add)
                if n:
                    dve.wait_ge(diff_done, s + 1)
                    v.tensor_tensor(square[:, 0:n], diff[:, 0:n], diff[:, 0:n], ALU.mult).then_inc(squares_done, 1)
                    dve.wait_ge(sums_done, s + 1)
                    v.tensor_scalar(scaled[:, 0:n], both[:, 0:n, 1], 1.0 / D, EPS, ALU.mult, ALU.add)\
                        .then_inc(scaled_done, 1)
                if k == 1:
                    e = bass.ds(in_pass(s, 1), 1)
                    v.tensor_tensor(idx_slots[:, e, :].rearrange("p a k -> p (a k)"), tg[:, p, :, 1],
                                    plain_rows[:, e, :].rearrange("p a k -> p (a k)"), ALU.min)
                if k2 == 1:
                    dve.wait_ge(carry_ready, 2 * (s - 2) + 2)
                    v.tensor_scalar(vv[:, 10:11], pse[2 * q][:, D + 1:D + 2], 1.0, None, ALU.add)
                    dve.wait_ge(ps_ready, 2 * (s - 2) + 8 + 2)
                    ins = v.tensor_scalar(vv[:, 11:12], pse[2 * q + 1][:, D + 1:D + 2], 1.0, None, ALU.add)
                if n:
                    dve.wait_ge(squares_done, s + 1)
                    dve.wait_ge(scaled_done, s + 1)
                    ins = v.scalar_tensor_tensor(vv[:, 0:n], square[:, 0:n], 0.25, scaled[:, 0:n], ALU.mult, ALU.add)
                if hi:
                    ins.then_inc(var_ready, 1)
                if kd["dense"][2]:
                    wait_past(dve, o_st[p2], 16 * i2)
                    add(s - 2, p2, 0)
                if hi:
                    dve.wait_ge(sqrt_ready, s + 1)
                    v.reciprocal(y[:, 0:hi], sq[:, q, 0:hi]).then_inc(recip_done, 1)
                if k == 2 and kd["first"][0]:
                    v.tensor_scalar(shift[:, :, :], idx_slots[:, :, :], float(T), float(2 * T), ALU.is_lt, ALU.mult)\
                        .then_inc(slots3_ready, 1)
                    dve.wait_ge(slots3_ready, 1)
                    v.tensor_tensor(idx_slots3[:, :, :], idx_slots[:, :, :], shift[:, :, :], ALU.add)\
                        .then_inc(slots3_ready, 1)
                if k:
                    dve.wait_ge(drow_ld[p], 16 * (i + 1))
                    dve.wait_ge(ps_ready, 2 * s + 2)
                    v.tensor_tensor(S[:, p, :, :], drow[:, p, :].rearrange("p (u e) -> p u e", u=2),
                                    col_sb[:, bass.ds(2 * in_pass(s, k), 2)].rearrange("p (u a) -> p u a", a=1)
                                    .broadcast_to([P, 2, P]), ALU.is_equal).then_inc(S_ready, 1)
                if hi:
                    dve.wait_ge(recip_done, s + 1)
                    v.scalar_tensor_tensor(yy[:, 0:hi], y[:, 0:hi], -0.5, y[:, 0:hi], ALU.mult, ALU.mult)\
                        .then_inc(recip2_done, 1)
                if hi:
                    dve.wait_ge(recip2_done, s + 1)
                    v.tensor_tensor(yyv[:, 0:hi], yy[:, 0:hi], vv[:, 0:hi], ALU.mult).then_inc(recip3_done, 1)
                if kd["dense"][2] and k == 1:
                    add(s - 2, p2, 1)
                if hi:
                    dve.wait_ge(recip3_done, s + 1)
                    named(v.scalar_tensor_tensor(rs[:, q, 0:hi], yyv[:, 0:hi], 1.5, y[:, 0:hi], ALU.add, ALU.mult),
                          rs_ready, s)
                if k == 1:
                    v.tensor_tensor(rs[:, q, 4:6], rs[:, q, 4:6], rs[:, q, 8:10], ALU.mult).then_inc(scale_ready, 1)
                    if k2 == 1:
                        keep(s - 2, q)
                    dve.wait_ge(scale_ready, s + 1)
                elif k2 == 1:
                    keep(s - 2, q)
                if n:
                    v.scalar_tensor_tensor(nb[:, q, 0:n], both[:, 0:n, 0], -0.5, rs[:, q, 0:n], ALU.mult, ALU.mult)\
                        .then_inc(nb_ready, 1)
                if k2:
                    update(s - 2, i2, p2, q, k2, kd)
                if kd["dense"][2] and k != 1:
                    add(s - 2, p2, 1)
                if k2 == 3:
                    dve.wait_ge(ttp_ready, 2 * in_pass(s - 2, 3) + 2)
                    wait_past(dve, fin_mm, in_pass(s - 2, 3))
                    v.tensor_copy(aT[0:3, :], tp[1][0:3, 2 * P:4 * P])
                    v.tensor_copy(tT[:, DC * P:2 * DC * P], tp[1][:, 0:DC * P]).then_inc(tT1_ready, 1)
                if kd["edge"][3] == 3:
                    dve.wait_ge(xd_ld[p3], 16 * (i3 - 2 * GS + 1))
                    wait_past(dve, out_sc[p3], 32 * (i3 - 2 * GS))
                    dve.wait_ge(o_st[p3], 16 * (DENSE // SLOTS))
                    dve.wait_ge(fin_mm, in_pass(s - 3, 3) + 1)
                    v.tensor_copy(scat[:, p3, :], idx_out[:, bass.ds(in_pass(s - 3, 3), 1), :]
                                  .rearrange("p a k -> p (a k)"))
                    for u in range(2):
                        last = v.scalar_tensor_tensor(
                            osb[:, p3, u, :], mm[p3 % 2][:, u * D:(u + 1) * D],
                            dinv_all[:, bass.ds(2 * in_pass(s - 3, 3) + u, 1)], xe[:, p3, 2 + u, :], ALU.mult, ALU.add)
                    last.then_inc(fin_ready, 1)

            def keep(s, q):
                v.tensor_copy(dinv_all[:, bass.ds(2 * s, 2)], rs[:, q, 10:12])

            def update(s, i, p, q, k, kd):
                cols = bass.ds(2 * in_pass(s, k), 2)
                if k < 3:
                    wait_past(dve, vout_ready, s - 1)
                else:
                    dve.wait_ge(vout_ready, 2 * STEPS)
                    wait_past(dve, ttp_ready, 2 * in_pass(s, 3) - 2)
                if k == 1:
                    v.tensor_tensor(inv[:, q, :], rs[:, q, 10:12], rs[:, q, 10:12], ALU.mult)
                else:
                    if k == 2:
                        v.tensor_tensor(inv[:, q, :], dinv_all[:, cols], dinv_all[:, cols], ALU.mult)
                    if k == 3 and kd["first"][2]:
                        v.reciprocal(root_all[:, :], dinv_all[:, :]).then_inc(root_ready, 1)
                        dve.wait_ge(root_ready, 1)
                        v.tensor_tensor(deg_all[:, :], root_all[:, :], root_all[:, :], ALU.mult).then_inc(root_ready, 1)
                        dve.wait_ge(root_ready, 2)
                    dve.wait_ge(own_ld[p], 16 * (i - GS + 1))
                    if k == 3:
                        v.tensor_tensor(al[:, q, :, 0:2], own[:, p, :, D:R],
                                        deg_all[:, cols].rearrange("p (u a) -> p u a", a=1).broadcast_to([P, 2, 2]),
                                        ALU.mult)
                        v.tensor_copy(al[:, q, :, 2], root_all[:, cols])
                for u in range(2):
                    if u == 1 and (kd["first"][1] or not kd["edge"][1]):
                        dve.wait_ge(ps_ready, 2 * s + 8 + 2)
                    else:
                        dve.wait_ge(carry_ready, 2 * s + 2 + u)
                    ps = pse[2 * q + u][:, 0:D + 1]
                    if k == 1:
                        last = v.scalar_tensor_tensor(t1[:, q, u, 0:D + 1], hd[:, p, u, 0:D + 1],
                                                      rs[:, q, 10 + u:11 + u], ps, ALU.mult, ALU.add)
                    else:
                        last = v.tensor_tensor(t1[:, q, u, 0:D + 1], ps, own[:, p, u, 0:D + 1], ALU.add)
                last.then_inc(t1_ready, 1)
            walk(dve, step)

            dve.wait_ge(s_inside, 1)
            n_inside = dve.value_load(inside[0:1, 0:1], min_val=0, max_val=E)
            with dve.If(n_inside > 0):
                for p in range(SLOTS):
                    dve.wait_ge(out_sc[p], 32 * GS)
                v.memset(osb[:, 0, 0:2, :], 0.0).then_inc(zero_ready, 1)
                with dve.Fori(0, HT) as t:
                    dve.wait_ge(key_ld, 16 * t + 16)
                    v.scalar_tensor_tensor(same_key[:, :], key_row[:, :], key[:, bass.ds(t, 1)], scanmat[:, 0:P],
                                           ALU.is_equal, ALU.mult).then_inc(same_ready, 1)
                    dve.wait_ge(same_ready, t + 1)
                    v.tensor_reduce(later[:, :], same_key[:, :], mybir.AxisListType.X, ALU.max).then_inc(later_ready, 1)
                    dve.wait_ge(later_ready, t + 1)
                    v.scalar_tensor_tensor(cell[:, bass.ds(t, 1)], later[:, :], BIG, key[:, bass.ds(t, 1)],
                                           ALU.mult, ALU.add).then_inc(cell_ready, 1)
                dve.wait_ge(zero_st, 16)
                with dve.Fori(0, DENSE) as t:
                    dve.wait_ge(l_x, 16 * t + 16)
                    for j in range(4):
                        last = v.bn_stats(st[:, j, :], xin[:, 0, j, :])
                    named(last, l_stats, t)
                    v.tensor_tensor(diff[:, 0:4], st[:, 0:4, 1], st[:, 0:4, 4], ALU.subtract)
                    named(v.tensor_tensor(both[:, 0:4, :], st[:, 0:4, 1:3], st[:, 0:4, 4:6], ALU.add), l_sums, t)
                    v.tensor_tensor(square[:, 0:4], diff[:, 0:4], diff[:, 0:4], ALU.mult)
                    named(v.tensor_scalar(scaled[:, 0:4], both[:, 0:4, 1], 1.0 / D, EPS, ALU.mult, ALU.add), l_squares, t)
                    v.scalar_tensor_tensor(vv[:, 0:4], square[:, 0:4], 0.25, scaled[:, 0:4], ALU.mult, ALU.add)\
                        .then_inc(l_var, 1)
                    dve.wait_ge(l_sqrt, t + 1)
                    named(v.reciprocal(y[:, 0:4], sq[:, 0, 0:4]), l_rs[0], t)
                    named(v.scalar_tensor_tensor(yy[:, 0:4], y[:, 0:4], -0.5, y[:, 0:4], ALU.mult, ALU.mult), l_rs[1], t)
                    named(v.tensor_tensor(yyv[:, 0:4], yy[:, 0:4], vv[:, 0:4], ALU.mult), l_rs[2], t)
                    named(v.scalar_tensor_tensor(rs[:, 0, 0:4], yyv[:, 0:4], 1.5, y[:, 0:4], ALU.add, ALU.mult), l_rs[3], t)
                    v.scalar_tensor_tensor(nb[:, 0, 0:4], both[:, 0:4, 0], -0.5, rs[:, 0, 0:4], ALU.mult, ALU.mult)\
                        .then_inc(l_nb, 1)
                    dve.wait_ge(l_mm, t + 1)
                    for k in range(2):
                        last = v.tensor_tensor(osb[:, 0, 2 * k:2 * k + 2, :], mm[k][:, :].rearrange("p (j d) -> p j d", j=2),
                                               xin[:, 0, 2 * k:2 * k + 2, :], ALU.add)
                    last.then_inc(l_add, 1)

        @block.scalar
        def _(act):
            a = nc.scalar
            act.sem_inc(norm_done, 4)

            act.wait_ge(s_pre, 1)
            a.activation(WT[1][:, :, :].rearrange("p c n -> p (c n)"), bank[0][:, :], ACT.Copy)
            a.activation(WT[0][:, :, :].rearrange("p c n -> p (c n)"), bank[1][:, :], ACT.Copy).then_inc(s_wt, 1)
            act.wait_ge(s_pre, 3)
            a.activation(W23[:, :, :].rearrange("p c n -> p (c n)"), bank[2][:, :], ACT.Copy).then_inc(s_wt, 1)
            act.wait_ge(s_pre, 4)
            a.activation(W123[:, :, :].rearrange("p c n -> p (c n)"), bank[3][:, :], ACT.Copy)
            a.activation(beta[0:1, 0:2, :].rearrange("p c n -> p (c n)"), bank[4][0:1, 0:2 * D], ACT.Copy).then_inc(s_wt, 1)
            act.wait_ge(s_beta, 1)
            act.dma_start(beta3[0:3, :], beta[0:1, :, :]).then_inc(s_rows, 16)
            for j in range(2):
                act.dma_start(bias_rhs[0:3, j * D:(j + 1) * D], bparts[0:1, :, :]).then_inc(s_rows, 16)

            def copy_row(frm, to):
                a.activation(to, frm, ACT.Copy).then_inc(carry_ready, 1)

            def update(s, i, p, q, k):
                if k == 1:
                    wait_past(act, v_st[1][p], 16 * i)
                else:
                    act.wait_ge(v_st[1][p], 16 * GS)
                    wait_past(act, v_st[2][p], 16 * (i - GS))
                act.wait_ge(t1_ready, s + 1 + 4)
                if k == 2:
                    a.activation(vout[:, p, :, D + 1:R], own[:, p, :, D:D + 1], ACT.Copy)
                for u in range(2):
                    last = a.activation(vout[:, p, u, 0:D + 1], t1[:, q, u, 0:D + 1], ACT.Copy,
                                        scale=inv[:, q, u:u + 1])
                last.then_inc(vout_ready, 1)

            def normalise(s, p, q):
                act.wait_ge(tp_ready, 2 * s + 2)
                act.wait_ge(nb_ready, s + 1)
                for j in range(4):
                    last = a.activation(xn[:, q, j, :], xin[:, p, j, :], ACT.Relu, scale=rs[:, q, j:j + 1],
                                        bias=nb[:, q, j:j + 1])
                last.then_inc(xn_ready, 1)

            def evac(s, q, k):
                act.wait_ge(tp_ready, 2 * s + k + 1 + 4)
                wait_past(act, mm_ready, 2 * s + k - 3)
                a.activation(hT[:, q, k, :], tp[k][:, :], ACT.Relu).then_inc(hT_ready, 1)

            def step(s, i, p, kd):
                q = p % 2
                (i1, p1), (i2, p2) = back(i, p, 1), back(i, p, 2)
                k, k1, k2 = kd["edge"][0:3]
                hi = 12 if k2 == 1 else 10 if k == 1 else 4 if kd["dense"][0] else 0
                if hi:
                    act.wait_ge(var_ready, s + 1)
                    a.activation(sq[:, q, 0:hi], vv[:, 0:hi], ACT.Sqrt).then_inc(sqrt_ready, 1)
                if k == 1:
                    act.dma_start(own_x[bass.ds(2 * P * s, 2 * P), :].rearrange("(u p) r -> p u r", p=P),
                                  xe[:, p, 2:4, :]).then_inc(ox_st[p], 16)
                if kd["first"][1]:
                    wait_past(act, carry_ready, 2 * (s - 1))
                    act.sem_inc(carry_ready, 1)
                    if k2:
                        update(s - 2, i2, p2, q, k2)
                if k1 and not kd["first"][1]:
                    if k1 > 1:
                        act.wait_ge(v_ld[p1], 32 * (i1 - GS + 1))
                    else:
                        act.wait_ge(norm_done, s + 4)
                    act.wait_ge(ps_ready, 2 * (s - 2) + 8 + 2)
                    copy_row(pse[2 * q + 1][0:1, 0:R], msg[0:1, p1, 0, :])
                if kd["dense"][1]:
                    evac(s - 1, p1 % 2, 0)
                    evac(s - 1, p1 % 2, 1)
                if kd["dense"][0] and k != 1:
                    normalise(s, p, q)
                if k2 == 3:
                    act.wait_ge(ttp_ready, 2 * in_pass(s - 2, 3) + 1)
                    wait_past(act, fin_mm, in_pass(s - 2, 3))
                    a.activation(tT[:, 0:DC * P], tp[0][:, 0:DC * P], ACT.Copy).then_inc(tT0_ready, 1)
                if k1:
                    if kd["first"][1] and k1 > 1:
                        act.wait_ge(v_ld[p1], 32 * (i1 - GS + 1))
                    if kd["first"][1] and k1 == 1:
                        act.wait_ge(norm_done, s + 4)
                    act.wait_ge(ps_ready, 2 * (s - 1) + 8 + 1)
                    copy_row(pse[2 * (p1 % 2)][0:1, 0:R], msg[0:1, p1, 1, :])
                if kd["dense"][0] and k == 1:
                    normalise(s, p, q)
                if k == 1:
                    wait_past(act, plain_st[p], 16 * i)
                    act.wait_ge(t1_ready, s + 1)
                    act.wait_ge(nb_ready, s + 1)
                    for j in range(4):
                        to = msg[:, p, j, 0:D] if j < 2 else hd[:, p, j - 2, 0:D]
                        a.activation(to, xe[:, p, j, :], ACT.Relu, scale=rs[:, q, 4 + j:5 + j], bias=nb[:, q, 4 + j:5 + j])
                    a.activation(msg[:, p, :, D], rs[:, q, 8:10], ACT.Copy).then_inc(norm_done, 1)
                if k2 in (1, 2) and not kd["first"][1]:
                    update(s - 2, i2, p2, q, k2)
            walk(act, step)

            act.wait_ge(s_inside, 1)
            n_inside = act.value_load(inside[0:1, 0:1], min_val=0, max_val=E)
            with act.If(n_inside > 0):
                with act.Fori(0, DENSE) as t:
                    act.wait_ge(l_var, t + 1)
                    a.activation(sq[:, 0, 0:4], vv[:, 0:4], ACT.Sqrt).then_inc(l_sqrt, 1)
                    act.wait_ge(l_nb, t + 1)
                    for j in range(4):
                        last = a.activation(xn[:, 0, j, :], xin[:, 0, j, :], ACT.Relu, scale=rs[:, 0, j:j + 1],
                                            bias=nb[:, 0, j:j + 1])
                    last.then_inc(l_xn, 1)
                    act.wait_ge(l_tp, t + 1)
                    for k in range(2):
                        last = a.activation(hT[:, 0, k, :], tp[k][:, :], ACT.Copy)
                    last.then_inc(l_hT, 1)

        @block.tensor
        def _(pe):
            t = nc.tensor
            pe.sem_inc(ps_ready, 8)
            pe.sem_inc(tp_ready, 4)
            pe.sem_inc(oh_used, RING)
            pe.wait_ge(s_const, 3)
            pe.wait_ge(s_w, 6 * 16)
            for w, b in ((W[1], 0), (W[0], 1)):
                for kc in range(DC):
                    for mc in range(DC):
                        o = (kc * DC + mc) * P
                        last = t.transpose(bank[b][:, o:o + P], w[:, mc, kc * P:(kc + 1) * P], ident[:, :])
            last.then_inc(s_pre, 1)

            def product(b, lhsT, rhs, wide):
                for mc in range(DC):
                    for kc in range(DC):
                        last = t.matmul(bank[b][:, mc * D:(mc + 1) * D], lhsT[:, kc, mc * P:(mc + 1) * P], rhs[:, kc, :],
                                        start=kc == 0, stop=kc == DC - 1)
                return last
            def histogram(i, j, start, stop):
                pe.wait_ge(oh_ready, RING * i + j + 1)
                t.matmul(bank[5][:, 0:HALF], olo[:, j, 0:P], ohi[:, j, :], start=start, stop=stop)
                t.matmul(bank[6][:, 0:HALF], olo[:, j, P:2 * P], ohi[:, j, :], start=start, stop=stop)\
                    .then_inc(oh_used, 1)
            for j in range(RING):
                histogram(0, j, j == 0, False)
            with pe.Fori(1, HT // RING - 1) as i:
                for j in range(RING):
                    histogram(i, j, False, False)
            for j in range(RING):
                histogram(HT // RING - 1, j, False, j == RING - 1)
            pe.wait_ge(s_hist, 1)
            pe.wait_ge(s_wt, 1)
            for c in range(HC):
                t.matmul(bank[c][:, 0:2 * P + 1], hist[:, c * P:(c + 1) * P], scanmat[:, :], start=True, stop=True)\
                    .then_inc(s_scan, 1)
            pe.wait_ge(s_banks, 1)
            t.matmul(bank[7][:, 0:HC], scanmat[:, 0:P], rowtot[:, :], start=True, stop=True)
            t.matmul(bank[7][:, 8:8 + HC], ones[:, :], rowtot[:, :], start=True, stop=True)
            t.matmul(bank[7][:, 16:17], ones[:, :], few[:, :], start=True, stop=True).then_inc(s_pre, 1)
            product(2, WT[1], W[2], D).then_inc(s_pre, 1)
            pe.wait_ge(s_wt, 2)
            product(3, WT[0], W23, D)
            for k, (o, w) in enumerate(((0, W23), (D, W[2]))):
                for kc in range(DC):
                    last = t.matmul(bank[4][0:1, o:o + D], bcol[:, k, kc:kc + 1], w[:, kc, :],
                                    start=kc == 0, stop=kc == DC - 1)
            last.then_inc(s_pre, 1)
            pe.wait_ge(s_wt, 3)
            pe.wait_ge(s_tab, 1)
            pe.wait_ge(s_rows, 3 * 16)

            def transposes(s, q, k):
                pe.wait_ge(xn_ready, s + 1)
                wait_past(pe, hT_ready, 2 * s + k - 1)
                for j in range(2):
                    for c in range(DC):
                        o = (j * DC + c) * P
                        last = t.transpose(tp[k][:, o:o + P], xn[:, q, 2 * k + j, c * P:(c + 1) * P], ident[:, :])
                last.then_inc(tp_ready, 1)

            def dense(s, q, k):
                pe.wait_ge(hT_ready, 2 * s + k + 1)
                pe.wait_ge(mm_used, 2 * s + 7 + k)
                t.matmul(mm[k][:, :], ones_b[:, :], bias_rhs[:, :], start=True, stop=False)
                for j in range(2):
                    for c in range(DC):
                        o = (j * DC + c) * P
                        last = t.matmul(mm[k][:, j * D:(j + 1) * D], hT[:, q, k, o:o + P], W123[:, c, :],
                                        start=False, stop=j == 1 and c == DC - 1)
                last.then_inc(mm_ready, 1)

            def sums(s, i, p, k, first, u):
                q = p % 2
                pe.wait_ge(S_ready, s + 4 + 1)
                if first and u == 0:
                    if k == 1:
                        pe.wait_ge(norm_done, s + 4 + 1)
                    else:
                        pe.wait_ge(v_ld[p], 32 * (i - GS + 1))
                pe.wait_ge(carry_ready, 2 * s + 1 + u)
                pe.wait_ge(t1_ready, s + 3)
                t.matmul(pse[2 * q + u][:, 0:R], S[:, p, u, :], msg[:, p, u, :], start=True, stop=True)\
                    .then_inc(ps_ready, 1)

            def step(s, i, p, kd):
                q = p % 2
                i1, p1 = back(i, p, 1)
                k1, k2 = kd["edge"][1], kd["edge"][2]
                if kd["dense"][1]:
                    transposes(s - 1, p1 % 2, 0)
                    transposes(s - 1, p1 % 2, 1)
                if kd["dense"][2]:
                    dense(s - 2, p % 2, 1)
                if k2 == 3:
                    pe.wait_ge(t1_ready, s - 2 + 4 + 1)
                    wait_past(pe, tT0_ready, in_pass(s - 2, 3))
                    wait_past(pe, tT1_ready, in_pass(s - 2, 3))
                    for c in range(DC):
                        last = t.transpose(tp[0][:, c * P:(c + 1) * P], t1[:, q, 0, c * P:(c + 1) * P], ident[:, :])
                    last.then_inc(ttp_ready, 1)
                    for u in range(2):
                        t.transpose(tp[1][0:3, (2 + u) * P:(3 + u) * P], al[:, q, u, 0:3], ident[:, :])
                    for c in range(DC):
                        last = t.transpose(tp[1][:, c * P:(c + 1) * P], t1[:, q, 1, c * P:(c + 1) * P], ident[:, :])
                    last.then_inc(ttp_ready, 1)
                if k1:
                    sums(s - 1, i1, p1, k1, kd["first"][1], 0)
                if kd["dense"][1]:
                    dense(s - 1, p1 % 2, 0)
                if k2 == 3:
                    pe.wait_ge(fin_ready, in_pass(s - 4, 3) + 1 + 4)
                    pe.wait_ge(tT0_ready, in_pass(s - 2, 3) + 1)
                    results(s - 2, q, 0)
                if k1:
                    sums(s - 1, i1, p1, k1, kd["first"][1], 1)
                if k2 == 3:
                    results(s - 2, q, 1).then_inc(fin_mm, 1)

            def results(s, q, u):
                for c in range(DC):
                    o = (u * DC + c) * P
                    t.matmul(mm[q][:, u * D:(u + 1) * D], tT[:, o:o + P], W123[:, c, :], start=c == 0, stop=False)
                if u == 0:
                    pe.wait_ge(tT1_ready, in_pass(s, 3) + 1)
                return t.matmul(mm[q][:, u * D:(u + 1) * D], aT[:, u * P:(u + 1) * P], beta3[:, :],
                                start=False, stop=True)
            walk(pe, step)

            pe.wait_ge(s_inside, 1)
            n_inside = pe.value_load(inside[0:1, 0:1], min_val=0, max_val=E)
            with pe.If(n_inside > 0):
                pe.wait_ge(wm_ld, 16)
                with pe.Fori(0, DENSE) as n:
                    pe.wait_ge(l_xn, n + 1)
                    for k in range(2):
                        for j in range(2):
                            for c in range(DC):
                                o = (j * DC + c) * P
                                last = t.transpose(tp[k][:, o:o + P], xn[:, 0, 2 * k + j, c * P:(c + 1) * P], ident[:, :])
                    last.then_inc(l_tp, 1)
                    pe.wait_ge(l_hT, n + 1)
                    for k in range(2):
                        for j in range(2):
                            for c in range(DC):
                                o = (j * DC + c) * P
                                last = t.matmul(mm[k][:, j * D:(j + 1) * D], hT[:, 0, k, o:o + P], Wm[:, c, :],
                                                start=c == 0, stop=c == DC - 1)
                    last.then_inc(l_mm, 1)


def kernel(**inputs):
    import numpy as np
    import concourse.bacc as bacc
    from concourse.bass_utils import run_bass_kernel_spmd

    x = np.asarray(inputs["x"])
    src, dst, weight = (np.asarray(inputs[n]) for n in ("src", "dst", "edge_weight"))
    xp = np.zeros((NP_, D), x.dtype)
    xp[:N] = x
    d = np.full(TILES * PER + 2, N, np.int32)
    d[0], d[1:E + 1], d[-1] = -1, dst, N + 2
    sr = np.full(TILES * PER + 2, N + 1, np.int32)
    sr[1:E + 1] = src
    tile = np.arange(TILES)[::-1, None] * PER + 1
    lane = np.arange(1, P)[None, :] - 1

    def tiles(first, others):
        return np.concatenate([first, others], axis=1)

    own = tiles(d[tile], d[tile + lane])
    prev = tiles(d[tile], d[tile + lane - 1])
    col = tiles(d[tile + PER], d[tile + lane])
    srcs = tiles(np.full((TILES, 1), N + 1, np.int32), sr[tile + lane])

    def by_tiles(a, fill):
        return np.ascontiguousarray(np.concatenate([a, np.full(HT * P - E, fill, a.dtype)]).reshape(HT, P).T)

    def steps(a):
        return a.reshape(STEPS, 2, P).transpose(2, 0, 1)

    arrays = {
        "x": xp,
        "idx_ends": np.ascontiguousarray(np.concatenate([steps(srcs), steps(own)], axis=2)),
        "prev_ends": np.ascontiguousarray(steps(prev)),
        "col_ends": np.ascontiguousarray(col.T),
        "row_ends": np.ascontiguousarray(own.reshape(1, TILES * P)),
        "dst_nat": by_tiles(dst, N),
        "src_nat": by_tiles(src, N),
        "weight_nat": by_tiles(weight, 0),
    }
    for n in ("W1", "b1", "W2", "b2", "W3", "b3"):
        a = np.asarray(inputs["L0_gnn_" + n])
        arrays[n] = np.ascontiguousarray(a.reshape(DC, P).T if n in ("b1", "b2") else a)
    nc = bacc.Bacc("TRN2", target_bir_lowering=False, num_devices=1)
    args = [nc.dram_tensor("in_" + n, a.shape, mybir.dt.from_np(a.dtype), kind="ExternalInput").ap()
            for n, a in arrays.items()]
    out = nc.dram_tensor("out", (NP_, D), F32, kind="ExternalOutput").ap()
    gnn(nc, *args, out)
    r = run_bass_kernel_spmd(nc, [{"in_" + n: a for n, a in arrays.items()}], core_ids=[0])
    return r.results[0]["out"][:N]
```
